# Optimizing a Trainium2 kernel written in Bass

```python
import numpy as np
import jax
import jax.numpy as jnp

def _softmax(x, axis=-1):
    return jax.nn.softmax(x, axis=axis)

def _gelu(x):
    return jax.nn.gelu(x, approximate=True)

def _silu(x):
    return jax.nn.silu(x)

def _sigmoid(x):
    return jax.nn.sigmoid(x)

def _layernorm(x, axis=-1, eps=1e-05):
    m = jnp.mean(x, axis=axis, keepdims=True)
    v = jnp.var(x, axis=axis, keepdims=True)
    return (x - m) / jnp.sqrt(v + eps)

def _scatter_add(tgt, idx, src, axis=0):
    return tgt.at[idx].add(src)

def _segment_sum(src, seg, n):
    return jax.ops.segment_sum(src, seg, n)
kernel_name = 'mk_conv_seq_d2_conv_nchw512_r2_3fd8e4'

def setup_inputs(seed: int=0):
    np.random.seed(seed)
    _w = jnp.asarray

    def _rec_inputs():
        import jax
        import jax.numpy as jnp
        _gk = jax.random.key(seed)
        x = -0.0006537 + 1.001 * jax.random.normal(jax.random.fold_in(_gk, 1), (2, 256, 48, 48), jnp.float32)
        return x
    x = _rec_inputs()

    def _L0_conv_setup():
        import jax, jax.numpy as jnp
        import numpy as np
        HEADS = 8
        DHEAD = 32
        TOPK = 64
        EPS = 1e-05

        def _conv1x1(x, Wm, b):
            return jnp.einsum('bchw,oc->bohw', x, Wm) + b[None, :, None, None]

        def _batchnorm(y, g, b):
            m = y.mean(axis=(0, 2, 3), keepdims=True)
            v = y.var(axis=(0, 2, 3), keepdims=True)
            return (y - m) * jax.lax.rsqrt(v + EPS) * g[None, :, None, None] + b[None, :, None, None]

        def _forward(x, Wq, bq, Wk, bk, Wv, bv, Wo, bo, W1, b1, g1, be1, W2, b2, g2, be2):
            B, C, H, W = x.shape
            N = H * W

            def heads(y):
                return y.reshape(B, HEADS, DHEAD, N).transpose(0, 1, 3, 2)
            q = heads(_conv1x1(x, Wq, bq))
            k = heads(_conv1x1(x, Wk, bk))
            v = heads(_conv1x1(x, Wv, bv))
            scores = jnp.einsum('bhnd,bhmd->bhnm', q, k) * DHEAD ** (-0.5)
            kth = jax.lax.top_k(scores, TOPK)[0][..., -1:]
            masked = jnp.where(scores >= kth, scores, jnp.finfo(scores.dtype).min)
            attn = jax.nn.softmax(masked, axis=-1)
            o = jnp.einsum('bhnm,bhmd->bhnd', attn, v)
            o = o.transpose(0, 1, 3, 2).reshape(B, C, H, W)
            o = _conv1x1(o, Wo, bo) + x
            h1 = jax.nn.relu(_batchnorm(_conv1x1(o, W1, b1), g1, be1))
            h2 = _batchnorm(_conv1x1(h1, W2, b2), g2, be2)
            return h2 + o
        key = jax.random.key(seed)
        ks = jax.random.split(key, 20)
        B, C, H, W = (2, 256, 48, 48)
        MLP = 1024

        def w(k, shape, fan_in):
            return (jax.random.normal(k, shape, jnp.float32) / np.sqrt(fan_in)).astype(jnp.float32)
        x = jax.random.normal(ks[0], (B, C, H, W), jnp.float32)
        return {'x': x, 'Wq': w(ks[1], (C, C), C), 'bq': jnp.zeros((C,), jnp.float32), 'Wk': w(ks[2], (C, C), C), 'bk': jnp.zeros((C,), jnp.float32), 'Wv': w(ks[3], (C, C), C), 'bv': jnp.zeros((C,), jnp.float32), 'Wo': w(ks[4], (C, C), C), 'bo': jnp.zeros((C,), jnp.float32), 'W1': w(ks[5], (MLP, C), C), 'b1': jnp.zeros((MLP,), jnp.float32), 'g1': jnp.ones((MLP,), jnp.float32), 'be1': jnp.zeros((MLP,), jnp.float32), 'W2': w(ks[6], (C, MLP), MLP), 'b2': jnp.zeros((C,), jnp.float32), 'g2': jnp.ones((C,), jnp.float32), 'be2': jnp.zeros((C,), jnp.float32)}
    _L0_conv_all = _L0_conv_setup()
    _L0_conv_in = {k: v for k, v in _L0_conv_all.items() if k in ('Wq', 'bq', 'Wk', 'bk', 'Wv', 'bv', 'Wo', 'bo', 'W1', 'b1', 'g1', 'be1', 'W2', 'b2', 'g2', 'be2')}
    del _L0_conv_all

    def _L1_conv_setup():
        import jax, jax.numpy as jnp
        import numpy as np
        HEADS = 8
        DIM_HEAD = 32
        key = jax.random.key(seed)
        k1, k2, k3 = jax.random.split(key, 3)
        dim = 256
        hidden = HEADS * DIM_HEAD
        x = jax.random.normal(k1, (2, dim, 48, 48), dtype=jnp.float32)
        g = jnp.ones((1, dim, 1, 1), dtype=jnp.float32)
        w_qkv = jax.random.normal(k2, (hidden * 3, dim), dtype=jnp.float32) * dim ** (-0.5)
        w_out = jax.random.normal(k3, (dim, hidden), dtype=jnp.float32) * hidden ** (-0.5)
        b_out = jnp.zeros((dim,), dtype=jnp.float32)
        return {'x': x, 'g': g, 'w_qkv': w_qkv, 'w_out': w_out, 'b_out': b_out}
    _L1_conv_all = _L1_conv_setup()
    _L1_conv_in = {k: v for k, v in _L1_conv_all.items() if k in ('g', 'w_qkv', 'w_out', 'b_out')}
    del _L1_conv_all
    return {'x': x, 'L0_conv_Wq': _L0_conv_in['Wq'], 'L0_conv_bq': _L0_conv_in['bq'], 'L0_conv_Wk': _L0_conv_in['Wk'], 'L0_conv_bk': _L0_conv_in['bk'], 'L0_conv_Wv': _L0_conv_in['Wv'], 'L0_conv_bv': _L0_conv_in['bv'], 'L0_conv_Wo': _L0_conv_in['Wo'], 'L0_conv_bo': _L0_conv_in['bo'], 'L0_conv_W1': _L0_conv_in['W1'], 'L0_conv_b1': _L0_conv_in['b1'], 'L0_conv_g1': _L0_conv_in['g1'], 'L0_conv_be1': _L0_conv_in['be1'], 'L0_conv_W2': _L0_conv_in['W2'], 'L0_conv_b2': _L0_conv_in['b2'], 'L0_conv_g2': _L0_conv_in['g2'], 'L0_conv_be2': _L0_conv_in['be2'], 'L1_conv_g': _L1_conv_in['g'], 'L1_conv_w_qkv': _L1_conv_in['w_qkv'], 'L1_conv_w_out': _L1_conv_in['w_out'], 'L1_conv_b_out': _L1_conv_in['b_out']}

def reference(x, L0_conv_Wq, L0_conv_bq, L0_conv_Wk, L0_conv_bk, L0_conv_Wv, L0_conv_bv, L0_conv_Wo, L0_conv_bo, L0_conv_W1, L0_conv_b1, L0_conv_g1, L0_conv_be1, L0_conv_W2, L0_conv_b2, L0_conv_g2, L0_conv_be2, L1_conv_g, L1_conv_w_qkv, L1_conv_w_out, L1_conv_b_out):
    import jax
    import jax.numpy as jnp

    def _L0_conv_ref(x, Wq, bq, Wk, bk, Wv, bv, Wo, bo, W1, b1, g1, be1, W2, b2, g2, be2):
        import jax, jax.numpy as jnp
        import numpy as np
        HEADS = 8
        DHEAD = 32
        TOPK = 64
        EPS = 1e-05

        def _conv1x1(x, Wm, b):
            return jnp.einsum('bchw,oc->bohw', x, Wm) + b[None, :, None, None]

        def _batchnorm(y, g, b):
            m = y.mean(axis=(0, 2, 3), keepdims=True)
            v = y.var(axis=(0, 2, 3), keepdims=True)
            return (y - m) * jax.lax.rsqrt(v + EPS) * g[None, :, None, None] + b[None, :, None, None]

        def _forward(x, Wq, bq, Wk, bk, Wv, bv, Wo, bo, W1, b1, g1, be1, W2, b2, g2, be2):
            B, C, H, W = x.shape
            N = H * W

            def heads(y):
                return y.reshape(B, HEADS, DHEAD, N).transpose(0, 1, 3, 2)
            q = heads(_conv1x1(x, Wq, bq))
            k = heads(_conv1x1(x, Wk, bk))
            v = heads(_conv1x1(x, Wv, bv))
            scores = jnp.einsum('bhnd,bhmd->bhnm', q, k) * DHEAD ** (-0.5)
            kth = jax.lax.top_k(scores, TOPK)[0][..., -1:]
            masked = jnp.where(scores >= kth, scores, jnp.finfo(scores.dtype).min)
            attn = jax.nn.softmax(masked, axis=-1)
            o = jnp.einsum('bhnm,bhmd->bhnd', attn, v)
            o = o.transpose(0, 1, 3, 2).reshape(B, C, H, W)
            o = _conv1x1(o, Wo, bo) + x
            h1 = jax.nn.relu(_batchnorm(_conv1x1(o, W1, b1), g1, be1))
            h2 = _batchnorm(_conv1x1(h1, W2, b2), g2, be2)
            return h2 + o
        return _forward(x, Wq, bq, Wk, bk, Wv, bv, Wo, bo, W1, b1, g1, be1, W2, b2, g2, be2)

    def _L1_conv_ref(x, g, w_qkv, w_out, b_out):
        import jax, jax.numpy as jnp
        import numpy as np
        HEADS = 8
        DIM_HEAD = 32
        b, c, H, W = x.shape
        N = H * W
        scale = DIM_HEAD ** (-0.5)
        l2 = jnp.sqrt(jnp.sum(x * x, axis=1, keepdims=True))
        xn = x / jnp.maximum(l2, 1e-12) * g * float(c) ** 0.5
        qkv = jnp.einsum('oc,bchw->bohw', w_qkv, xn)
        q, k, v = jnp.split(qkv, 3, axis=1)
        rs = lambda t: t.reshape(b, HEADS, DIM_HEAD, N)
        q, k, v = (rs(q) * scale, rs(k), rs(v))
        sim = jnp.einsum('bhdi,bhdj->bhij', q, k)
        attn = jax.nn.softmax(sim, axis=-1)
        out = jnp.einsum('bhij,bhdj->bhdi', attn, v)
        out = out.reshape(b, HEADS * DIM_HEAD, H, W)
        return jnp.einsum('oc,bchw->bohw', w_out, out) + b_out[None, :, None, None] + x

    def _gn(v, G=32, eps=1e-05):
        B_, C_, H_, W_ = v.shape
        g = v.reshape(B_, G, C_ // G, H_, W_)
        m = jnp.mean(g, axis=(2, 3, 4), keepdims=True)
        s = jnp.var(g, axis=(2, 3, 4), keepdims=True)
        return ((g - m) / jnp.sqrt(s + eps)).reshape(v.shape)

    def _ln_c(v, eps=1e-06):
        m = jnp.mean(v, axis=1, keepdims=True)
        s = jnp.var(v, axis=1, keepdims=True)
        return (v - m) / jnp.sqrt(s + eps)

    def _ln_t(v, eps=1e-05):
        m = jnp.mean(v, axis=-1, keepdims=True)
        s = jnp.var(v, axis=-1, keepdims=True)
        return (v - m) / jnp.sqrt(s + eps)

    def _to_tokens(v):
        B_, C_, H_, W_ = v.shape
        return v.reshape(B_, C_, H_ * W_).transpose(0, 2, 1)

    def _from_tokens(t, like):
        B_, C_, H_, W_ = like.shape
        return t.transpose(0, 2, 1).reshape(B_, C_, H_, W_)
    x = _L0_conv_ref(x, L0_conv_Wq, L0_conv_bq, L0_conv_Wk, L0_conv_bk, L0_conv_Wv, L0_conv_bv, L0_conv_Wo, L0_conv_bo, L0_conv_W1, L0_conv_b1, L0_conv_g1, L0_conv_be1, L0_conv_W2, L0_conv_b2, L0_conv_g2, L0_conv_be2)
    x = _L1_conv_ref(x, L1_conv_g, L1_conv_w_qkv, L1_conv_w_out, L1_conv_b_out)
    return x

_drawn_inputs = setup_inputs


def setup_inputs(seed=0):
    import zlib

    import numpy as np

    out = dict(_drawn_inputs(seed))
    spreads = {'L0_conv_bq': (0.0, 0.1),
     'L0_conv_bk': (0.0, 0.1),
     'L0_conv_bv': (0.0, 0.1),
     'L0_conv_bo': (0.0, 0.1),
     'L0_conv_b1': (0.0, 0.1),
     'L0_conv_g1': (1.0, 0.2),
     'L0_conv_be1': (0.0, 0.1),
     'L0_conv_b2': (0.0, 0.1),
     'L0_conv_g2': (1.0, 0.2),
     'L0_conv_be2': (0.0, 0.1),
     'L1_conv_g': (1.0, 0.2),
     'L1_conv_b_out': (0.0, 0.1)}
    factors = {}
    for name, (base, spread) in spreads.items():
        noise = np.random.default_rng([zlib.crc32(name.encode()), seed]).standard_normal(out[name].shape)
        drawn = base * np.exp(spread * noise) if base else spread * noise
        out[name] = jnp.asarray(drawn.astype(out[name].dtype))
    for name, factor in factors.items():
        out[name] = (out[name] * factor).astype(out[name].dtype)
    return out
```

```python
from contextlib import ExitStack

import numpy as np
import concourse.bass as bass
from concourse import mybir

F32 = mybir.dt.float32
F32R = mybir.dt.float32r
I32 = mybir.dt.int32
ALU = mybir.AluOpType
ACT = mybir.ActivationFunctionType
AX = mybir.AxisListType

P = 128
B, C, N = 2, 256, 48 * 48
KC = C // P
HEADS, D = 8, 32
MLP = 1024
MT = MLP // P
TOPK = 64
BN_EPS = 1e-5
SCALE = float(D) ** -0.5
BANK = 512

PAIR = 2 * P
PAIRS = N // PAIR
MCH = N // P
PRE = 6
PCOLS = N // PRE
PM = PCOLS // P
HEAD_STEPS = B * HEADS
ALL_PAIRS = HEAD_STEPS * PAIRS

CHUNK = 48
CHUNKS = N // CHUNK
KEEP = 4
CAND = CHUNKS * KEEP + 8
ROUNDS = TOPK // 8
LOWEST = -3.0e38
STEEP = 2.0 ** 60

SCOLS = [(c, min(BANK, N - c)) for c in range(0, N, BANK)]
TGROUPS = [(m, min(4, MCH - m)) for m in range(0, MCH, 4)]
NTG = len(TGROUPS)


def cols(start, n):
    return slice(start, start + n) if isinstance(start, int) else bass.ds(start, n)


class Tally:
    semaphore = None


def wait_alone(engine, semaphore, value):
    engine.wait_ge(semaphore, value)
    engine.sem_inc(Tally.semaphore, 1)


def constants(nc, ctx):
    sb = lambda name, shape, dt=F32: ctx.enter_context(nc.sbuf_tensor(name, shape, dt))
    k = {
        "ident": sb("ident", [P, P]),
        "ones": sb("ones", [P, P]),
        "ones_r": sb("ones_r", [P, P], F32R),
        "k_low": sb("k_low", [P, 1]),
        "q_low": sb("q_low", [P, 1]),
    }
    made = ctx.enter_context(nc.semaphore("constants_made"))
    Tally.semaphore = ctx.enter_context(nc.semaphore("waits_alone"))
    with nc.Block() as block:

        @block.gpsimd
        def _(pool):
            pool.memset(k["ident"][:, :], 0.0).then_inc(made, 1)
            pool.wait_ge(made, 1)
            pool.affine_select(out=k["ident"][:, :], in_=k["ident"][:, :], compare_op=ALU.not_equal,
                               fill=1.0, base=0, pattern=[[-1, P]], channel_multiplier=1)

        @block.vector
        def _(dve):
            dve.memset(k["ones"][:, :], 1.0)
            dve.memset(k["ones_r"][:, :].bitcast(F32), 1.0)
            for quadrant in range(4):
                rows = slice(D * quadrant, D * quadrant + D)
                dve.memset(k["k_low"][rows, :], float(quadrant >= 2))
                dve.memset(k["q_low"][rows, :], float(quadrant % 2))
    return k


def over_steps(engine, step):
    with engine.Fori(0, HEADS) as h:
        for b in range(B):
            head = h * B + b
            with engine.Fori(0, PRE // 2) as half:
                for r in range(2):
                    step(head * PAIRS + half * 2 + r, half * 2 + r, (b + r) % 2, h, b, head)
            for i in range(PRE, PAIRS):
                step(head * PAIRS + i, i, (b + i) % 2, h, b, head)


class BankUses:

    def __init__(self, av, before):
        self.plain, self.preparing, self.before = av + 1, av + 4, before
        self.head = PAIRS * self.plain + 3 * PRE

    def __call__(self, head, i):
        if isinstance(i, int) and i >= PRE:
            return head * self.head + self.before + PRE * self.preparing + (i - PRE) * self.plain
        return head * self.head + self.before + i * self.preparing


def load_projections(sync, w_s, drams, h, loaded):
    for t, w in zip(w_s, drams):
        for r in range(t.shape[2] // D):
            sync.dma_start(t[:, :, D * r:D * r + D], w[h]).then_inc(loaded, 16)


class Shared:

    def __init__(self, nc, ctx, cst, xs, name, ahead, uses):
        sb = lambda n, shape, dt=F32: ctx.enter_context(nc.sbuf_tensor(name + n, shape, dt))
        sem = lambda n: ctx.enter_context(nc.semaphore(name + n))
        self.cst, self.xs, self.uses = cst, xs, uses
        self.ahead = ahead
        self.wq_s, self.wk_s, self.wv_s = sb("wq", [P, KC, 4 * D]), sb("wk", [P, KC, 4 * D]), sb("wv", [P, KC, D])
        self.bq_s, self.bk_s, self.bv_s = sb("bq", [P, HEADS + 1]), sb("bk", [P, HEADS + 1]), sb("bv", [D, HEADS + 1])
        self.k_raw, self.k_part = sb("k_raw", [P, PCOLS]), sb("k_part", [P, PCOLS], F32R)
        self.q_raw, self.q_part = sb("q_raw", [P, PAIR]), sb("q_part", [P, PAIR], F32R)
        self.k_stack = [sb(f"k_stack{n}", [P, N], F32R) for n in range(2)]
        self.q_stack = [sb(f"q_stack{n}", [P, PAIR], F32R) for n in range(2)]
        self.v_cols = sb("v_cols", [D, PCOLS])
        self.o_head = [sb(f"o_head{n}", [D, N]) for n in range(2)]
        self.bank = ctx.enter_context(nc.psum_tensor(name + "bank", [P, BANK], F32))
        self.x_loaded, self.bias_loaded = sem("x_loaded"), sem("bias_loaded")
        self.wq_loaded, self.wkv_loaded = sem("wq_loaded"), sem("wkv_loaded")
        self.buffers_set = sem("buffers_set")
        self.bank_filled, self.bank_kept = sem("bank_filled"), sem("bank_kept")
        self.k_stack_ready, self.q_stack_ready = sem("k_stack_ready"), sem("q_stack_ready")
        self.o_ready, self.o_stored = sem("o_ready"), sem("o_stored")
        self.pool_order = sem("pool_order")

    def load_first(self, sync, w_q, w_k, w_v, biases):
        load_projections(sync, (self.wk_s, self.wv_s), (w_k, w_v), 0, self.wkv_loaded)
        load_projections(sync, (self.wq_s,), (w_q,), 0, self.wq_loaded)
        if biases:
            sync.wait_ge(self.buffers_set, 1)
            for t, src in zip((self.bq_s, self.bk_s, self.bv_s), biases):
                for r in range(t.shape[0] // D):
                    sync.dma_start(t[D * r:D * r + D, 0:HEADS],
                                   src).then_inc(self.bias_loaded, 16)

    def load_and_store(self, sync, w_q, w_k, w_v, ao):
        sync.sem_inc(self.o_stored, 32)

        def store(h, b):
            sync.wait_ge(self.o_ready, (h * B + b + 1) * PAIRS)
            sync.dma_start(ao.rearrange("(h d) n -> h d n", d=D)[h, :, b * N:b * N + N],
                           self.o_head[b][:, :]).then_inc(self.o_stored, 16)

        def per_head(h, h_next):
            sync.wait_ge(self.bank_filled, self.uses(h * B, PRE))
            load_projections(sync, (self.wk_s, self.wv_s), (w_k, w_v), h_next, self.wkv_loaded)
            store(h, 0)
            sync.wait_ge(self.bank_filled, self.uses(h * B + 1, PAIRS - self.ahead))
            load_projections(sync, (self.wq_s,), (w_q,), h_next, self.wq_loaded)
            store(h, 1)

        with sync.Fori(0, HEADS - 1) as h:
            per_head(h, h + 1)
        per_head(HEADS - 1, HEADS - 1)
        sync.wait_ge(self.o_stored, 32 + 16 * HEAD_STEPS)

    def bank_free(self, pe, use):
        if not (isinstance(use, int) and use == 0):
            wait_alone(pe, self.bank_kept, use)

    def project(self, pe, use, out, weights, b, col, n):
        self.bank_free(pe, use)
        for kc in range(KC):
            last = pe.matmul(out, weights[:, kc, :], self.xs[:, kc, b, cols(col, n)],
                             start=kc == 0, stop=kc == KC - 1)
        last.then_inc(self.bank_filled, 1)

    def project_q(self, pe, use, b, i):
        self.project(pe, use, self.bank[:, 0:PAIR], self.wq_s, b, i * PAIR, PAIR)

    def project_k(self, pe, use, b, c):
        self.project(pe, use, self.bank[:, 0:PCOLS], self.wk_s, b, c * PCOLS, PCOLS)

    def project_v(self, pe, use, b, c):
        self.project(pe, use, self.bank[0:D, 0:PCOLS], self.wv_s, b, c * PCOLS, PCOLS)

    def turn_v(self, pe, use):
        self.bank_free(pe, use)
        for m in range(PM):
            last = pe.transpose(self.bank[:, D * m:D * m + D], self.v_cols[:, P * m:P * m + P],
                                self.cst["ident"][0:D, 0:D])
        last.then_inc(self.bank_filled, 1)

    def keep(self, act, use, out, rows, n, bias):
        wait_alone(act, self.bank_filled, use + 1)
        act.activation(out, self.bank[0:rows, 0:n], ACT.Identity, bias=bias).then_inc(self.bank_kept, 1)

    def keep_q(self, act, use, h, pairs_before):
        if not (isinstance(pairs_before, int) and pairs_before == 0):
            act.wait_ge(self.q_stack_ready, pairs_before)
        self.keep(act, use, self.q_raw[:, :], P, PAIR, self.bq_s[:, cols(h, 1)])

    def keep_k(self, act, use, h, chunks_before):
        if not (isinstance(chunks_before, int) and chunks_before == 0):
            act.wait_ge(self.k_stack_ready, chunks_before)
        self.keep(act, use, self.k_raw[:, :], P, PCOLS, self.bk_s[:, cols(h, 1)])

    def keep_v(self, act, use, h):
        self.keep(act, use, self.v_cols[:, :], D, PCOLS, self.bv_s[:, cols(h, 1)])

    def split(self, pool, raw, low, part, out, order, done):
        pool.tensor_scalar(part, raw, 0.0, low[:, 0:1], ALU.add, ALU.mult).then_inc(self.pool_order, 1)
        pool.wait_ge(self.pool_order, order)
        pool.tensor_tensor(out, raw, part.bitcast(F32), ALU.subtract).then_inc(done, 1)

    def split_k(self, pool, use, b, c, order):
        wait_alone(pool, self.bank_kept, use + 1)
        self.split(pool, self.k_raw[:, :], self.cst["k_low"], self.k_part[:, :],
                   self.k_stack[b][:, cols(c * PCOLS, PCOLS)], order, self.k_stack_ready)

    def split_q(self, pool, use, parity, order):
        wait_alone(pool, self.bank_kept, use + 1)
        self.split(pool, self.q_raw[:, :], self.cst["q_low"], self.q_part[:, :],
                   self.q_stack[parity][:, :], order, self.q_stack_ready)


def attention_top(nc, cst, xs, x, w_q, w_k, w_v, b_q, b_k, b_v, ao):
    ctx = ExitStack()
    with ctx:
        sb = lambda name, shape, dt=F32: ctx.enter_context(nc.sbuf_tensor("a_" + name, shape, dt))
        sem = lambda name: ctx.enter_context(nc.semaphore("a_" + name))
        uses = BankUses(av=2, before=3 * PRE + 3)
        sh = Shared(nc, ctx, cst, xs, "a_", 3, uses)
        v_ones = [sb(f"v_ones{n}", [P, MCH, 2 * D]) for n in range(2)]
        scores = [sb(f"scores{n}", [P, N]) for n in range(4)]
        probs = [sb(f"probs{n}", [P, N]) for n in range(2)]
        probs_t = [sb(f"probs_t{n}", [P, MCH, P]) for n in range(2)]
        scratch = sb("scratch", [P, N])
        top8 = sb("top8", [P, 2, CHUNKS + 1, 8])
        cand = sb("cand", [P, 2, CAND])
        best = sb("best", [P, 2, TOPK])
        missed = sb("missed", [P, 2])
        flag, flag_t, flags = sb("flag", [P, D]), sb("flag_t", [P, D]), sb("flags", [1, P])
        any_missed = sb("any_missed", [1, 1], I32)
        steep_kth = [sb(f"steep_kth{n}", [P, 2]) for n in range(2)]
        minus_max = [sb(f"minus_max{n}", [P, 2]) for n in range(2)]
        av = [sb(f"av{n}", [2 * D, PAIR]) for n in range(2)]
        rden = [sb(f"rden{n}", [D, PAIR]) for n in range(2)]

        ps_s = ctx.enter_context(nc.psum_tensor("a_ps_s", [P, 5 * BANK], F32))
        ps_t = [ctx.enter_context(nc.psum_tensor(f"a_ps_t{n}", [P, BANK], F32)) for n in range(2)]

        scores_done, scores_kept = sem("scores_done"), sem("scores_kept")
        kth_ready = sem("kth_ready")
        penalty_ready, masked_ready, probs_ready = sem("penalty_ready"), sem("masked_ready"), sem("probs_ready")
        turned, turned_kept = sem("turned"), sem("turned_kept")
        rden_ready = sem("rden_ready")
        tops_taken, dve_order = sem("tops_taken"), sem("dve_order")

        block = ctx.enter_context(nc.Block())

        @block.sync
        def _(sync):
            for b in range(B):
                for kc in range(KC):
                    sync.dma_start(xs[:, kc, b, :], x[b, kc * P:kc * P + P, :]).then_inc(sh.x_loaded, 16)
            sh.load_first(sync, w_q, w_k, w_v, (b_q, b_k, b_v))
            sh.load_and_store(sync, w_q, w_k, w_v, ao)

        @block.tensor
        def _(pe):
            def score(tile, u, parity, b, first=False):
                if not first:
                    pe.wait_ge(scores_kept, tile)
                for c, n in SCOLS:
                    last = pe.matmul(ps_s[:, c:c + n], sh.q_stack[parity][:, P * u:P * u + P],
                                     sh.k_stack[b][:, c:c + n], start=True, stop=True)
                last.then_inc(scores_done, 1)

            def turn(u, g):
                m0, n = TGROUPS[g]
                bank = ps_t[(NTG * u + g) % 2]
                for m in range(n):
                    last = pe.transpose(bank[:, P * m:P * m + P], probs[u][:, P * (m0 + m):P * (m0 + m) + P],
                                        cst["ident"][:, :])
                last.then_inc(turned, 1)

            def output(tile, u, b, use):
                pe.wait_ge(probs_ready, tile + 1)
                turn(u, 0)
                turn(u, 1)
                sh.bank_free(pe, use)
                for g, (m0, n) in enumerate(TGROUPS):
                    pe.wait_ge(turned_kept, tile * NTG + g + 1)
                    for m in range(m0, m0 + n):
                        last = pe.matmul(sh.bank[0:2 * D, 0:P], v_ones[b][:, m, :], probs_t[u][:, m, :],
                                         start=m == 0, stop=m == MCH - 1)
                    if g + 2 < NTG:
                        turn(u, g + 2)
                last.then_inc(sh.bank_filled, 1)

            pe.wait_ge(sh.x_loaded, 16 * B * KC)
            pe.wait_ge(sh.wkv_loaded, 80)
            for c in range(PRE):
                sh.project_k(pe, 3 * c, 0, c)
                sh.project_v(pe, 3 * c + 1, 0, c)
                sh.turn_v(pe, 3 * c + 2)
            pe.wait_ge(sh.wq_loaded, 64)
            for n in range(3):
                sh.project_q(pe, 3 * PRE + n, 0, n)
            pe.wait_ge(sh.k_stack_ready, PRE)
            for n in range(2):
                pe.wait_ge(sh.q_stack_ready, n + 1)
                for u in range(2):
                    score(2 * n + u, u, n, 0, first=n + u == 0)

            def step(pair, i, parity, h, b, head):
                use = uses(head, i)
                tail = isinstance(i, int)
                scored_b = 1 - b if tail and i + 2 >= PAIRS else b
                output(2 * pair, 0, b, use)
                if scored_b != b:
                    pe.wait_ge(sh.k_stack_ready, (head + 2) * PRE)
                pe.wait_ge(sh.q_stack_ready, pair + 3)
                score(2 * pair + 4, 0, parity, scored_b)
                output(2 * pair + 1, 1, b, use + 1)
                score(2 * pair + 5, 1, parity, scored_b)
                if tail and i + 3 == PAIRS:
                    pe.wait_ge(sh.wq_loaded, 64 * (h + b + 1))
                if tail and i + 3 >= PAIRS:
                    sh.project_q(pe, use + 2, 1 - b, i + 3 - PAIRS)
                else:
                    sh.project_q(pe, use + 2, b, i + 3)
                if not tail:
                    pe.wait_ge(sh.wkv_loaded, 80 * (h + b + 1))
                    sh.project_k(pe, use + 3, 1 - b, i)
                    sh.project_v(pe, use + 4, 1 - b, i)
                    sh.turn_v(pe, use + 5)

            over_steps(pe, step)

        @block.scalar
        def _(act):
            def keep_turned_v(use, b, c):
                wait_alone(act, sh.bank_filled, use + 1)
                act.activation(v_ones[b][:, cols(c * PM, PM), 0:D],
                               sh.bank[:, 0:PM * D].rearrange("p (m d) -> p m d", d=D),
                               ACT.Copy).then_inc(sh.bank_kept, 1)

            def keep_scores(tile, n):
                act.wait_ge(scores_done, tile + 1)
                act.activation(scores[n][:, :], ps_s[:, 0:N], ACT.Copy).then_inc(scores_kept, 1)

            act.wait_ge(sh.bias_loaded, 16 * 9)
            act.wait_ge(sh.buffers_set, 1)
            for c in range(PRE):
                sh.keep_k(act, 3 * c, 0, c)
                sh.keep_v(act, 3 * c + 1, 0)
                keep_turned_v(3 * c + 2, 0, c)
            for n in range(3):
                sh.keep_q(act, 3 * PRE + n, 0, n)
            for n in range(4):
                keep_scores(n, n)

            def output(tile, u, parity, use):
                act.wait_ge(masked_ready, tile + 1)
                act.activation(probs[u][:, :], probs[u][:, :], ACT.Exp, scale=SCALE,
                               bias=minus_max[parity][:, u:u + 1]).then_inc(probs_ready, 1)
                for g, (m0, n) in enumerate(TGROUPS):
                    act.wait_ge(turned, tile * NTG + g + 1)
                    act.activation(probs_t[u][:, m0:m0 + n, :],
                                   ps_t[(NTG * u + g) % 2][:, 0:n * P].rearrange("p (m q) -> p m q", q=P),
                                   ACT.Copy).then_inc(turned_kept, 1)
                act.wait_ge(sh.bank_filled, use + 1)
                act.activation(av[parity][:, P * u:P * u + P], sh.bank[0:2 * D, 0:P],
                               ACT.Copy).then_inc(sh.bank_kept, 1)

            def step(pair, i, parity, h, b, head):
                use = uses(head, i)
                tail = isinstance(i, int)
                act.wait_ge(kth_ready, pair + 1)
                for u in range(2):
                    act.activation(probs[u][:, :], scores[2 * parity + u][:, :], ACT.Relu, scale=-STEEP,
                                   bias=steep_kth[parity][:, u:u + 1]).then_inc(penalty_ready, 1)
                act.wait_ge(sh.o_ready, pair)
                output(2 * pair, 0, parity, use)
                keep_scores(2 * pair + 4, 2 * parity)
                output(2 * pair + 1, 1, parity, use + 1)
                keep_scores(2 * pair + 5, 2 * parity + 1)
                sh.keep_q(act, use + 2, h + b if tail and i + 3 >= PAIRS else h, pair + 3)
                if not tail:
                    sh.keep_k(act, use + 3, h + b, (head + 1) * PRE + i)
                    sh.keep_v(act, use + 4, h + b)
                    keep_turned_v(use + 5, 1 - b, i)

            over_steps(act, step)

        @block.gpsimd
        def _(pool):
            for c in range(PRE):
                sh.split_k(pool, 3 * c, 0, c, c + 1)
            for n in range(3):
                if n == 2:
                    pool.wait_ge(scores_done, 2)
                sh.split_q(pool, 3 * PRE + n, n % 2, PRE + n + 1)

            def step(pair, i, parity, h, b, head):
                use = uses(head, i)
                tail = isinstance(i, int)
                splits = PRE + 3 + head * (PAIRS + PRE) + (PRE + i if tail else i * 2)
                for u in range(2):
                    pool.wait_ge(penalty_ready, 2 * pair + u + 1)
                    pool.tensor_tensor(probs[u][:, :], scores[2 * parity + u][:, :], probs[u][:, :],
                                       ALU.subtract).then_inc(masked_ready, 1)
                pool.wait_ge(scores_done, 2 * pair + 4)
                sh.split_q(pool, use + 2, 1 - parity, splits + 1)
                if not tail:
                    sh.split_k(pool, use + 3, 1 - b, i, splits + 2)
                pool.wait_ge(rden_ready, pair + 1)
                pool.wait_ge(sh.o_stored, 16 * (head + 1))
                pool.tensor_tensor(sh.o_head[b][:, cols(i * PAIR, PAIR)], av[parity][0:D, :],
                                   rden[parity][:, :], ALU.mult).then_inc(sh.o_ready, 1)

            over_steps(pool, step)

        @block.vector
        def _(dve):
            at = {"n": 0}

            def counted(instruction):
                at["n"] += 1
                instruction.then_inc(dve_order, 1)
                return at["n"]

            def chunk_tops(pair, parity, u, between=lambda c: None):
                wait_alone(dve, scores_kept, 2 * pair + u + 1)
                for c in range(CHUNKS):
                    last = dve.max(top8[:, u, c, :], scores[2 * parity + u][:, CHUNK * c:CHUNK * c + CHUNK])
                    if c < CHUNKS - 1:
                        between(c)
                last.then_inc(tops_taken, 1)

            def select(pair):
                at["n"] = 0
                after = lambda n: dve.wait_ge(dve_order, n)
                wait_alone(dve, tops_taken, 2 * pair + 2)
                rest, written = [0, 0], [0, 0]
                for u in range(2):
                    rest[u] = counted(dve.max(top8[:, u, CHUNKS, :], top8[:, u, 0:CHUNKS, KEEP:8]))
                    counted(dve.tensor_copy(cand[:, u, 0:CHUNKS * KEEP].rearrange("p (c k) -> p c k", k=KEEP),
                                            top8[:, u, 0:CHUNKS, 0:KEEP]))
                for u in range(2):
                    after(rest[u])
                    written[u] = counted(dve.tensor_copy(cand[:, u, CHUNKS * KEEP:CAND], top8[:, u, CHUNKS, :]))
                counted(dve.tensor_reduce(missed[:, :], top8[:, :, :, 7], AX.X, ALU.max))
                for r in range(ROUNDS):
                    found = [0, 0]
                    for u in range(2):
                        after(written[u])
                        found[u] = counted(dve.max(best[:, u, 8 * r:8 * r + 8], cand[:, u, :]))
                    if r < ROUNDS - 1:
                        for u in range(2):
                            after(found[u])
                            written[u] = counted(dve.match_replace(cand[:, u, :], best[:, u, 8 * r:8 * r + 8],
                                                                   cand[:, u, :], LOWEST))

            def check(pair, c):
                after = lambda: dve.wait_ge(dve_order, at["n"])
                if c == 1:
                    after()
                    counted(dve.tensor_tensor(missed[:, :], missed[:, :], best[:, :, TOPK - 1], ALU.is_gt))
                elif c == 3:
                    after()
                    counted(dve.tensor_reduce(flag[:, 0:1], missed[:, :], AX.X, ALU.max))
                elif c == 5:
                    after()
                    counted(dve.transpose(flag_t[:, :], flag[:, :]))
                elif c == 7:
                    after()
                    for q in range(4):
                        last = dve.tensor_copy(flags[:, D * q:D * q + D], flag_t[D * q:D * q + 1, :])
                    counted(last)
                elif c == 9:
                    after()
                    counted(dve.tensor_reduce(any_missed[:, :], flags[:, :], AX.X, ALU.max))

            def hand_on(pair, parity):
                dve.wait_ge(dve_order, at["n"])
                again = dve.value_load(any_missed[0:1, 0:1], min_val=0, max_val=1)
                dve.sem_clear(dve_order)
                with dve.If(again > 0):
                    for u in range(2):
                        dve.tensor_copy(scratch[:, :], scores[2 * parity + u][:, :])
                        for r in range(ROUNDS):
                            dve.drain()
                            dve.max(best[:, u, 8 * r:8 * r + 8], scratch[:, :])
                            dve.drain()
                            if r < ROUNDS - 1:
                                dve.match_replace(scratch[:, :], best[:, u, 8 * r:8 * r + 8], scratch[:, :],
                                                  LOWEST)
                dve.tensor_scalar(steep_kth[parity][:, :], best[:, :, TOPK - 1], STEEP, None, ALU.mult)
                dve.tensor_scalar(minus_max[parity][:, :], best[:, :, 0], -SCALE, None,
                                  ALU.mult).then_inc(kth_ready, 1)

            def reciprocals(pair, parity):
                dve.wait_ge(scores_kept, 2 * pair + 6)
                dve.reciprocal(rden[parity][:, :], av[parity][D:2 * D, :]).then_inc(rden_ready, 1)

            def pair_step(pair, parity):
                chunk_tops(pair, parity, 1)
                select(pair)
                chunk_tops(pair + 1, 1 - parity, 0, lambda c: check(pair, c))
                hand_on(pair, parity)

            for t in (sh.bq_s, sh.bk_s, sh.bv_s, flag):
                dve.memset(t[:, :], 0.0)
            for t in v_ones:
                last = dve.memset(t[:, :, :], 1.0)
            last.then_inc(sh.buffers_set, 1)
            dve.wait_ge(sh.buffers_set, 1)
            chunk_tops(0, 0, 0)
            pair_step(0, 0)
            with dve.Fori(0, (ALL_PAIRS - 2) // 2) as k:
                pair_step(k * 2 + 1, 1)
                reciprocals(k * 2, 0)
                pair_step(k * 2 + 2, 0)
                reciprocals(k * 2 + 1, 1)
            pair_step(ALL_PAIRS - 1, 1)
            reciprocals(ALL_PAIRS - 2, 0)
            reciprocals(ALL_PAIRS - 1, 1)


def mlp(nc, cst, xs, ao, x1, w_o, b_o, w_1, b_1, g_1, be_1, w_2, b_2, g_2, be_2, g_rms):
    CW = BANK
    NCH = B * N // CW
    ctx = ExitStack()
    with ctx:
        sb = lambda name, shape, dt=F32: ctx.enter_context(nc.sbuf_tensor("m_" + name, shape, dt))
        sem = lambda name: ctx.enter_context(nc.semaphore("m_" + name))
        hid = sb("hid", [P, NCH, MT, CW])
        w = sb("w", [P, KC * MLP])
        w1_s = w[:, :].rearrange("p (k m) -> p k m", k=KC)
        w2_s = w[:, :].rearrange("p (k c) -> p k c", k=MT)
        wo_s = sb("wo", [P, KC, C])
        vec = {n: sb(n, [P, m]) for n, m in (("b_o", KC), ("b_1", MT), ("g_1", MT), ("be_1", MT), ("b_2", KC),
                                             ("g_2", KC), ("be_2", KC), ("g_rms", KC))}
        stats1, mean1 = sb("stats1", [P, MT, NCH * 6]), sb("mean1", [P, MT, 2])
        stats2, mean2 = sb("stats2", [P, KC, NCH * 6]), sb("mean2", [P, KC, 2])
        scale1, shift1 = sb("scale1", [P, MT]), sb("shift1", [P, MT])
        scale2, shift2 = sb("scale2", [P, KC]), sb("shift2", [P, KC])
        ps_o = ctx.enter_context(nc.psum_tensor("m_ps_o", [P, KC, BANK], F32))
        ps_h = [ctx.enter_context(nc.psum_tensor(f"m_ps_h{n}", [P, BANK], F32)) for n in range(4)]
        xf = xs[:, :, :, :].rearrange("p k b n -> p k (b n)")

        first_ao_loaded, ao_loaded = sem("first_ao_loaded"), sem("ao_loaded")
        w1_loaded, w2_loaded, vec_loaded = sem("w1_loaded"), sem("w2_loaded"), sem("vec_loaded")
        proj_done, o_ready = sem("proj_done"), sem("o_ready")
        hid_done, hid_kept = sem("hid_done"), sem("hid_kept")
        var1_ready, dev1_ready, bn1_ready, bn_order = (sem("var1_ready"), sem("dev1_ready"), sem("bn1_ready"),
                                                       sem("bn_order"))
        relu_done, y_done, y_kept = sem("relu_done"), sem("y_done"), sem("y_kept")
        var2_ready, dev2_ready, bn2_ready = sem("var2_ready"), sem("dev2_ready"), sem("bn2_ready")
        y_scaled, x1_ready, x1_stored = sem("y_scaled"), sem("x1_ready"), sem("x1_stored")
        squares_ready, sums_done, norm_ready = sem("squares_ready"), sem("sums_done"), sem("norm_ready")
        xn_order, xn_ready = sem("xn_order"), sem("xn_ready")
        block = ctx.enter_context(nc.Block())

        def ao_slot(c, n):
            return hid[:, cols(c, n), MT - KC:MT, :]

        @block.sync
        def _(sync):
            sync.dma_start(wo_s[:, :, :], w_o.rearrange("(k p) o -> p k o", p=P)).then_inc(first_ao_loaded, 16)
            for kc in range(KC):
                src = ao[kc * P:kc * P + P, :].rearrange("p (c n) -> p c n", n=CW)
                sync.dma_start(hid[:, 0, MT - KC + kc, :], src[:, 0, :]).then_inc(first_ao_loaded, 16)
            for kc in range(KC):
                src = ao[kc * P:kc * P + P, :].rearrange("p (c n) -> p c n", n=CW)
                sync.dma_start(hid[:, 1:NCH, MT - KC + kc, :], src[:, 1:NCH, :]).then_inc(ao_loaded, 16)
            sync.dma_start(w1_s, w_1.rearrange("(k p) o -> p k o", p=P)).then_inc(w1_loaded, 16)
            for name, src in (("b_o", b_o), ("b_1", b_1), ("g_1", g_1), ("be_1", be_1), ("b_2", b_2),
                              ("g_2", g_2), ("be_2", be_2), ("g_rms", g_rms)):
                sync.dma_start(vec[name][:, :], src).then_inc(vec_loaded, 16)
            sync.wait_ge(hid_done, NCH * MT)
            sync.dma_start(w2_s, w_2.rearrange("(k p) o -> p k o", p=P)).then_inc(w2_loaded, 16)
            sync.wait_ge(x1_ready, NCH)
            for kc in range(KC):
                sync.dma_start(x1[kc * P:kc * P + P, :].rearrange("p (c n) -> p c n", n=CW),
                               hid[:, :, kc, :]).then_inc(x1_stored, 16)
            sync.wait_ge(x1_stored, 16 * KC)

        @block.tensor
        def _(pe):
            def project(c):
                pe.wait_ge(o_ready, c)
                for oc in range(KC):
                    for kc in range(KC):
                        last = pe.matmul(ps_o[:, oc, :], wo_s[:, kc, P * oc:P * oc + P],
                                         hid[:, c, MT - KC + kc, :], start=kc == 0, stop=kc == KC - 1)
                last.then_inc(proj_done, 1)

            def hidden(c):
                pe.wait_ge(o_ready, c + 1)
                for mt in range(MT):
                    pe.wait_ge(hid_kept, c * MT + mt + 1)
                    for kc in range(KC):
                        last = pe.matmul(ps_h[mt % 4][:, :], w1_s[:, kc, P * mt:P * mt + P],
                                         xf[:, kc, cols(c * CW, CW)], start=kc == 0, stop=kc == KC - 1)
                    last.then_inc(hid_done, 1)

            pe.wait_ge(first_ao_loaded, 16 * 3)
            for oc in range(KC):
                for kc in range(KC):
                    last = pe.matmul(ps_o[:, oc, :], wo_s[:, kc, P * oc:P * oc + P], hid[:, 0, MT - KC + kc, :],
                                     start=kc == 0, stop=kc == KC - 1)
            last.then_inc(proj_done, 1)
            pe.wait_ge(ao_loaded, 16 * KC)
            pe.wait_ge(w1_loaded, 16)
            with pe.Fori(0, NCH - 1) as c:
                project(c + 1)
                hidden(c)
            hidden(NCH - 1)

            pe.wait_ge(w2_loaded, 16)
            with pe.Fori(0, NCH) as c:
                for oc in range(KC):
                    pe.wait_ge(y_kept, c * KC + oc + 1)
                    for mt in range(MT):
                        if oc == 0:
                            pe.wait_ge(relu_done, c * MT + mt + 1)
                        last = pe.matmul(ps_o[:, oc, :], w2_s[:, mt, P * oc:P * oc + P], hid[:, c, mt, :],
                                         start=mt == 0, stop=mt == MT - 1)
                    last.then_inc(y_done, 1)

            with pe.Fori(0, NCH) as c:
                pe.wait_ge(squares_ready, c + 1)
                pe.wait_ge(norm_ready, c + 1)
                for kc in range(KC):
                    last = pe.matmul(ps_h[0][:, :], cst["ones"][:, :], hid[:, c, KC + kc, :],
                                     start=kc == 0, stop=kc == KC - 1)
                last.then_inc(sums_done, 1)

        @block.scalar
        def _(act):
            act.sem_inc(hid_kept, 4)
            act.sem_inc(y_kept, KC)
            act.sem_inc(norm_ready, 1)
            act.wait_ge(vec_loaded, 16 * 8)
            with act.Fori(0, NCH) as c:
                for mt in range(MT):
                    act.wait_ge(hid_done, c * MT + mt + 1)
                    act.activation(hid[:, c, mt, :], ps_h[mt % 4][:, :], ACT.Identity,
                                   bias=vec["b_1"][:, mt:mt + 1]).then_inc(hid_kept, 1)
            act.wait_ge(var1_ready, 1)
            act.activation(mean1[:, :, 1], mean1[:, :, 1], ACT.Sqrt).then_inc(dev1_ready, 1)
            act.wait_ge(bn1_ready, 1)

            def relu(c):
                for mt in range(MT):
                    act.activation(hid[:, c, mt, :], hid[:, c, mt, :], ACT.Relu, scale=scale1[:, mt:mt + 1],
                                   bias=shift1[:, mt:mt + 1]).then_inc(relu_done, 1)

            def keep_y(c):
                for oc in range(KC):
                    act.wait_ge(y_done, c * KC + KC)
                    act.activation(hid[:, c, oc, :], ps_o[:, oc, :], ACT.Identity,
                                   bias=vec["b_2"][:, oc:oc + 1]).then_inc(y_kept, 1)

            relu(0)
            with act.Fori(0, NCH - 1) as c:
                relu(c + 1)
                keep_y(c)
            keep_y(NCH - 1)
            act.wait_ge(var2_ready, 1)
            act.activation(mean2[:, :, 1], mean2[:, :, 1], ACT.Sqrt).then_inc(dev2_ready, 1)
            act.wait_ge(bn2_ready, 1)
            with act.Fori(0, NCH) as c:
                for kc in range(KC):
                    last = act.activation(hid[:, c, kc, :], hid[:, c, kc, :], ACT.Identity,
                                          scale=scale2[:, kc:kc + 1], bias=shift2[:, kc:kc + 1])
                last.then_inc(y_scaled, 1)
            with act.Fori(0, NCH) as c:
                act.wait_ge(x1_ready, c + 1)
                act.activation(hid[:, c, KC:2 * KC, :], hid[:, c, 0:KC, :], ACT.Square).then_inc(squares_ready, 1)
            with act.Fori(0, NCH) as c:
                act.wait_ge(sums_done, c + 1)
                act.activation(hid[:, c, 2 * KC, :], ps_h[0][:, :], ACT.Sqrt).then_inc(norm_ready, 1)

        @block.vector
        def _(dve):
            def residual(c):
                dve.wait_ge(proj_done, c + 1)
                for oc in range(KC):
                    x_c = xf[:, oc, cols(c * CW, CW)]
                    last = dve.scalar_tensor_tensor(x_c, ps_o[:, oc, :], vec["b_o"][:, oc:oc + 1], x_c,
                                                    ALU.add, ALU.add)
                last.then_inc(o_ready, 1)

            def hidden_stats(c):
                for mt in range(MT):
                    dve.wait_ge(hid_kept, c * MT + mt + 5)
                    last = dve.bn_stats(stats1[:, mt, cols(c * 6, 6)], hid[:, c, mt, :])
                return last

            def batchnorm(blocks, stats, mean, gamma, beta, scale, shift, var_ready, dev_ready, ready, order):
                for m in range(blocks):
                    last = dve.bn_aggr(mean[:, m, :], stats[:, m, :])
                last.then_inc(bn_order, 1)
                dve.wait_ge(bn_order, order + 1)
                dve.tensor_scalar(mean[:, :, 1], mean[:, :, 1], BN_EPS, None, ALU.add).then_inc(var_ready, 1)
                dve.wait_ge(dev_ready, 1)
                dve.reciprocal(scale[:, :], mean[:, :, 1]).then_inc(bn_order, 1)
                dve.wait_ge(bn_order, order + 2)
                dve.tensor_tensor(scale[:, :], scale[:, :], gamma[:, :], ALU.mult).then_inc(bn_order, 1)
                dve.wait_ge(bn_order, order + 3)
                dve.tensor_tensor(shift[:, :], mean[:, :, 0], scale[:, :], ALU.mult).then_inc(bn_order, 1)
                dve.wait_ge(bn_order, order + 4)
                dve.tensor_tensor(shift[:, :], beta[:, :], shift[:, :], ALU.subtract).then_inc(ready, 1)

            dve.wait_ge(vec_loaded, 16 * 8)
            residual(0)
            with dve.Fori(0, NCH - 1) as c:
                residual(c + 1)
                hidden_stats(c)
            hidden_stats(NCH - 1).then_inc(bn_order, 1)
            dve.wait_ge(bn_order, 1)
            batchnorm(MT, stats1, mean1, vec["g_1"], vec["be_1"], scale1, shift1, var1_ready, dev1_ready,
                      bn1_ready, 1)
            with dve.Fori(0, NCH) as c:
                for oc in range(KC):
                    dve.wait_ge(y_kept, c * KC + oc + 1 + KC)
                    dve.bn_stats(stats2[:, oc, cols(c * 6, 6)], hid[:, c, oc, :]).then_inc(xn_order, 1)
            dve.wait_ge(xn_order, NCH * KC)
            batchnorm(KC, stats2, mean2, vec["g_2"], vec["be_2"], scale2, shift2, var2_ready, dev2_ready,
                      bn2_ready, 5)
            with dve.Fori(0, NCH) as c:
                dve.wait_ge(y_scaled, c + 1)
                dve.tensor_tensor(hid[:, c, 0:KC, :], hid[:, c, 0:KC, :], xf[:, :, cols(c * CW, CW)],
                                  ALU.add).then_inc(x1_ready, 1)
            base = NCH * KC
            with dve.Fori(0, NCH) as c:
                norm = hid[:, c, 2 * KC, :]
                dve.wait_ge(norm_ready, c + 2)
                dve.tensor_scalar(norm, norm, 1e-12, None, ALU.max).then_inc(xn_order, 1)
                wait_alone(dve, xn_order, base + c * 2 + 1)
                dve.reciprocal(norm, norm).then_inc(xn_order, 1)
                dve.wait_ge(xn_order, base + c * 2 + 2)
                for kc in range(KC):
                    dve.scalar_tensor_tensor(xf[:, kc, cols(c * CW, CW)], hid[:, c, kc, :],
                                             vec["g_rms"][:, kc:kc + 1], norm, ALU.mult, ALU.mult)
            xn = xf[:, :, :]
            dve.drain()
            dve.tensor_scalar(xn, xn, float(C) ** 0.5, None, ALU.mult).then_inc(xn_ready, 1)
            dve.wait_ge(xn_ready, 1)


def attention_full(nc, cst, xs, w_q, w_k, w_v, ao):
    ctx = ExitStack()
    with ctx:
        sb = lambda name, shape, dt=F32: ctx.enter_context(nc.sbuf_tensor("b_" + name, shape, dt))
        sem = lambda name: ctx.enter_context(nc.semaphore("b_" + name))
        GROUPS, PER = MCH // 2, 2
        uses = BankUses(av=1, before=3 * PRE + 2)
        sh = Shared(nc, ctx, cst, xs, "b_", 2, uses)
        v_raw = sb("v_raw", [P, PM, D])
        v_stack = [sb(f"v_stack{n}", [P, MCH, 3 * D], F32R) for n in range(2)]
        expo = [sb(f"expo{n}", [P, MCH, PAIR]) for n in range(2)]
        high, low = sb("high", [P, MCH, PAIR], F32R), sb("low", [P, MCH, PAIR], F32R)
        row_max = sb("row_max", [P, 2])
        minus_max = [sb(f"minus_max{n}", [P, PAIR], F32R) for n in range(2)]
        av_high, av_low, av_sum = sb("av_high", [D, PAIR]), sb("av_low", [D, PAIR]), sb("av_sum", [D, PAIR])
        rden = sb("rden", [D, PAIR])

        ps_s = ctx.enter_context(nc.psum_tensor("b_ps_s", [P, 5 * BANK], F32))
        ps_t = [ctx.enter_context(nc.psum_tensor(f"b_ps_t{n}", [P, PER, PAIR], F32)) for n in range(2)]

        scores_done, max_ready, diagonal_ready = sem("scores_done"), sem("max_ready"), sem("diagonal_ready")
        shifted_done, expo_ready = sem("shifted_done"), sem("expo_ready")
        high_ready, low_ready = sem("high_ready"), sem("low_ready")
        v_split = sem("v_split")
        rden_ready = sem("rden_ready")

        block = ctx.enter_context(nc.Block())

        @block.sync
        def _(sync):
            sh.load_first(sync, w_q, w_k, w_v, None)
            sh.load_and_store(sync, w_q, w_k, w_v, ao)

        @block.tensor
        def _(pe):
            def score(tile, u, parity, b, first=False):
                if not first:
                    pe.wait_ge(max_ready, tile)
                for c, n in SCOLS:
                    last = pe.matmul(ps_s[:, c:c + n], sh.q_stack[parity][:, P * u:P * u + P],
                                     sh.k_stack[b][:, c:c + n], start=True, stop=True)
                last.then_inc(scores_done, 1)

            def shifted(pair, g, parity, b):
                bank = ps_t[(parity + g) % 2]
                if g == 0:
                    pe.wait_ge(diagonal_ready, pair + 1)
                pe.wait_ge(expo_ready, pair * GROUPS + g + 1)
                for m in range(PER):
                    block_of_k = sh.k_stack[b][:, P * (PER * g + m):P * (PER * g + m) + P]
                    pe.matmul(bank[:, m, :], cst["ones_r"][:, :], minus_max[parity][:, :], start=True, stop=False)
                    last = pe.matmul(bank[:, m, :], block_of_k, sh.q_stack[parity][:, :], start=False, stop=True)
                last.then_inc(shifted_done, 1)

            def weigh(pair, g, b):
                pe.wait_ge(low_ready, pair * GROUPS + g + 1)
                for m in range(PER * g, PER * g + PER):
                    for part in (high, low):
                        last = pe.matmul(sh.bank[0:3 * D, 0:PAIR], v_stack[b][:, m, :], part[:, m, :],
                                         start=m == 0 and part is high, stop=m == MCH - 1 and part is low)
                return last

            pe.wait_ge(sh.wkv_loaded, 80)
            for c in range(PRE):
                sh.project_k(pe, 3 * c, 0, c)
                sh.project_v(pe, 3 * c + 1, 0, c)
                sh.turn_v(pe, 3 * c + 2)
            pe.wait_ge(sh.wq_loaded, 64)
            for n in range(2):
                sh.project_q(pe, 3 * PRE + n, 0, n)
            pe.wait_ge(sh.k_stack_ready, PRE)
            pe.wait_ge(sh.q_stack_ready, 1)
            for u in range(2):
                score(u, u, 0, 0, first=u == 0)
            for g in range(2):
                shifted(0, g, 0, 0)

            def step(pair, i, parity, h, b, head):
                use = uses(head, i)
                tail = isinstance(i, int)
                last_step = tail and i == PAIRS - 1
                next_b = 1 - b if last_step else b
                if tail and i + 2 == PAIRS:
                    pe.wait_ge(sh.wq_loaded, 64 * (h + b + 1))
                if tail and i + 2 >= PAIRS:
                    sh.project_q(pe, use, 1 - b, i + 2 - PAIRS)
                else:
                    sh.project_q(pe, use, b, i + 2)
                shifted(pair, 2, parity, b)
                if last_step:
                    pe.wait_ge(sh.k_stack_ready, (head + 2) * PRE)
                pe.wait_ge(sh.q_stack_ready, pair + 2)
                score(2 * pair + 2, 0, 1 - parity, next_b)
                shifted(pair, 3, parity, b)
                if not tail:
                    pe.wait_ge(sh.wkv_loaded, 80 * (h + b + 1))
                    sh.project_k(pe, use + 1, 1 - b, i)
                shifted(pair, 4, parity, b)
                if not tail:
                    sh.project_v(pe, use + 2, 1 - b, i)
                shifted(pair, 5, parity, b)
                if not tail:
                    sh.turn_v(pe, use + 3)
                score(2 * pair + 3, 1, 1 - parity, next_b)
                sh.bank_free(pe, use + 1 if tail else use + 4)
                pe.wait_ge(v_split, (head + 1) * PRE)
                weigh(pair, 0, b)
                for g in range(6, GROUPS):
                    shifted(pair, g, parity, b)
                    weigh(pair, 2 * g - 11, b)
                    weigh(pair, 2 * g - 10, b)
                for g in range(2):
                    shifted(pair + 1, g, 1 - parity, next_b)
                weigh(pair, 7, b)
                weigh(pair, 8, b).then_inc(sh.bank_filled, 1)

            over_steps(pe, step)

        @block.scalar
        def _(act):
            act.sem_inc(expo_ready, 2)

            def keep_turned_v(use, b, c):
                wait_alone(act, sh.bank_filled, use + 1)
                turned = sh.bank[:, 0:PM * D].rearrange("p (m d) -> p m d", d=D)
                act.activation(v_stack[b][:, cols(c * PM, PM), 0:D], turned, ACT.Copy)
                act.activation(v_raw[:, :, :], turned, ACT.Copy).then_inc(sh.bank_kept, 1)

            def exponentials(pair, g, parity):
                act.wait_ge(shifted_done, pair * GROUPS + g + 1)
                act.activation(expo[parity][:, PER * g:PER * g + PER, :], ps_t[(parity + g) % 2][:, :, :],
                               ACT.Exp, scale=SCALE).then_inc(expo_ready, 1)

            act.wait_ge(sh.buffers_set, 1)
            for c in range(PRE):
                sh.keep_k(act, 3 * c, 0, c)
                sh.keep_v(act, 3 * c + 1, 0)
                if c:
                    act.wait_ge(v_split, c)
                keep_turned_v(3 * c + 2, 0, c)
            for n in range(2):
                sh.keep_q(act, 3 * PRE + n, 0, n)
            for g in range(2):
                exponentials(0, g, 0)

            def step(pair, i, parity, h, b, head):
                use = uses(head, i)
                tail = isinstance(i, int)
                sh.keep_q(act, use, h + b if tail and i + 2 >= PAIRS else h, pair + 2)
                exponentials(pair, 2, parity)
                exponentials(pair, 3, parity)
                if not tail:
                    sh.keep_k(act, use + 1, h + b, (head + 1) * PRE + i)
                exponentials(pair, 4, parity)
                if not tail:
                    sh.keep_v(act, use + 2, h + b)
                exponentials(pair, 5, parity)
                if not tail:
                    act.wait_ge(v_split, (head + 1) * PRE + i)
                    keep_turned_v(use + 3, 1 - b, i)
                for g in range(6, GROUPS):
                    exponentials(pair, g, parity)
                for g in range(2):
                    exponentials(pair + 1, g, 1 - parity)
                act.wait_ge(sh.o_ready, pair)
                act.wait_ge(sh.bank_filled, (use + 1 if tail else use + 4) + 1)
                for n, t in enumerate((av_high, av_low, av_sum)):
                    last = act.activation(t[:, :], sh.bank[D * n:D * n + D, 0:PAIR], ACT.Copy)
                last.then_inc(sh.bank_kept, 1)

            over_steps(act, step)


        @block.gpsimd
        def _(pool):
            def split_v(use, b, c):
                wait_alone(pool, sh.bank_kept, use + 1)
                v_high = v_stack[b][:, cols(c * PM, PM), 0:D]
                pool.tensor_tensor(v_stack[b][:, cols(c * PM, PM), D:2 * D], v_raw[:, :, :],
                                   v_high.bitcast(F32), ALU.subtract).then_inc(v_split, 1)

            def low_part(pair, g, parity):
                pool.wait_ge(high_ready, pair * GROUPS + g + 1)
                blocks = slice(PER * g, PER * g + PER)
                pool.tensor_tensor(low[:, blocks, :], expo[parity][:, blocks, :], high[:, blocks, :].bitcast(F32),
                                   ALU.subtract).then_inc(low_ready, 1)

            for c in range(PRE):
                sh.split_k(pool, 3 * c, 0, c, c + 1)
                split_v(3 * c + 2, 0, c)
            for n in range(2):
                sh.split_q(pool, 3 * PRE + n, n, PRE + n + 1)

            def step(pair, i, parity, h, b, head):
                use = uses(head, i)
                tail = isinstance(i, int)
                order = PRE + 2 + head * (2 * PAIRS + PRE) + (PRE + i * 2 if tail else i * 3)
                for g in range(4):
                    low_part(pair, g, parity)
                if not tail:
                    sh.split_k(pool, use + 1, 1 - b, i, order + 1)
                for g in range(4, 6):
                    low_part(pair, g, parity)
                if not tail:
                    split_v(use + 3, 1 - b, i)
                    order = order + 1
                for g in range(6, GROUPS):
                    low_part(pair, g, parity)
                pool.wait_ge(shifted_done, pair * GROUPS + GROUPS)
                sh.split_q(pool, use, parity, order + 1)
                pool.wait_ge(rden_ready, pair + 1)
                pool.tensor_tensor(av_high[:, :], av_high[:, :], av_low[:, :], ALU.add).then_inc(sh.pool_order, 1)
                pool.wait_ge(sh.pool_order, order + 2)
                pool.wait_ge(sh.o_stored, 16 * (head + 1))
                pool.tensor_tensor(sh.o_head[b][:, cols(i * PAIR, PAIR)], av_high[:, :], rden[:, :],
                                   ALU.mult).then_inc(sh.o_ready, 1)

            over_steps(pool, step)

        @block.vector
        def _(dve):
            def high_part(pair, g, parity):
                dve.wait_ge(expo_ready, pair * GROUPS + g + 3)
                blocks = slice(PER * g, PER * g + PER)
                dve.tensor_copy(high[:, blocks, :], expo[parity][:, blocks, :]).then_inc(high_ready, 1)

            def maximum(tile, u):
                dve.wait_ge(scores_done, tile + 1)
                dve.tensor_reduce(row_max[:, u:u + 1], ps_s[:, 0:N], AX.X, ALU.max).then_inc(max_ready, 1)

            def diagonals(pair, parity):
                dve.wait_ge(max_ready, 2 * pair + 2)
                for u in range(2):
                    last = dve.tensor_scalar(minus_max[parity][:, P * u:P * u + P], cst["ident"][:, :],
                                             row_max[:, u:u + 1], -1.0, ALU.mult, ALU.mult)
                last.then_inc(diagonal_ready, 1)

            for t in (sh.bq_s, sh.bk_s, sh.bv_s):
                dve.memset(t[:, :], 0.0)
            for t in v_stack:
                last = dve.memset(t[:, :, 2 * D:3 * D].bitcast(F32), 1.0)
            last.then_inc(sh.buffers_set, 1)
            for u in range(2):
                maximum(u, u)
            diagonals(0, 0)

            def step(pair, i, parity, h, b, head):
                use = uses(head, i)
                tail = isinstance(i, int)
                dve.wait_ge(sh.bank_filled, use)
                for g in range(3):
                    high_part(pair, g, parity)
                maximum(2 * pair + 2, 0)
                for g in range(3, 6):
                    high_part(pair, g, parity)
                maximum(2 * pair + 3, 1)
                diagonals(pair + 1, 1 - parity)
                for g in range(6, GROUPS):
                    high_part(pair, g, parity)
                dve.wait_ge(sh.bank_kept, (use + 1 if tail else use + 4) + 1)
                dve.reciprocal(rden[:, :], av_sum[:, :]).then_inc(rden_ready, 1)

            over_steps(dve, step)


def output(nc, xs, ao, x1, w_out, b_out, out):
    CW = N // PRE
    CHB = N // CW
    ctx = ExitStack()
    with ctx:
        sb = lambda name, shape, dt=F32: ctx.enter_context(nc.sbuf_tensor("o_" + name, shape, dt))
        sem = lambda name: ctx.enter_context(nc.semaphore("o_" + name))
        w, bias = sb("w", [P, KC, C]), sb("bias", [P, KC])
        a, y = sb("a", [P, KC, B * N]), sb("y", [P, KC, B * N])
        ps = ctx.enter_context(nc.psum_tensor("o_ps", [P, KC, BANK], F32))
        w_loaded, a_loaded = sem("w_loaded"), [sem(f"a_loaded{b}") for b in range(B)]
        proj_done, added, stored = sem("proj_done"), sem("added"), sem("stored")
        block = ctx.enter_context(nc.Block())

        @block.sync
        def _(sync):
            sync.dma_start(w[:, :, :], w_out.rearrange("(k p) o -> p k o", p=P)).then_inc(w_loaded, 16)
            sync.dma_start(bias[:, :], b_out).then_inc(w_loaded, 16)
            for b in range(B):
                for kc in range(KC):
                    for t, src in ((a, ao), (y, x1)):
                        sync.dma_start(t[:, kc, b * N:b * N + N],
                                       src[kc * P:kc * P + P, b * N:b * N + N]).then_inc(a_loaded[b], 16)
            for b in range(B):
                with sync.Fori(0, CHB) as c:
                    sync.wait_ge(added, c + b * CHB + 1)
                    sync.dma_start(out[b].rearrange("(k p) n -> p k n", p=P)[:, :, cols(c * CW, CW)],
                                   y[:, :, cols(c * CW + b * N, CW)]).then_inc(stored, 16)
            sync.wait_ge(stored, 16 * B * CHB)

        @block.tensor
        def _(pe):
            pe.wait_ge(w_loaded, 32)
            for b in range(B):
                pe.wait_ge(a_loaded[b], 64)
                with pe.Fori(0, CHB) as c:
                    pe.wait_ge(added, c + b * CHB)
                    for oc in range(KC):
                        for kc in range(KC):
                            last = pe.matmul(ps[:, oc, 0:CW], w[:, kc, P * oc:P * oc + P],
                                             a[:, kc, cols(c * CW + b * N, CW)], start=kc == 0, stop=kc == KC - 1)
                    last.then_inc(proj_done, 1)

        @block.vector
        def _(dve):
            dve.wait_ge(w_loaded, 32)
            for b in range(B):
                dve.wait_ge(a_loaded[b], 64)
                with dve.Fori(0, CHB) as c:
                    dve.wait_ge(proj_done, c + b * CHB + 1)
                    for oc in range(KC):
                        y_c = y[:, oc, cols(c * CW + b * N, CW)]
                        last = dve.scalar_tensor_tensor(y_c, ps[:, oc, 0:CW], bias[:, oc:oc + 1], y_c,
                                                        ALU.add, ALU.add)
                    last.then_inc(added, 1)


def build(nc, t, out, stop=None):
    ao0 = nc.dram_tensor("ao0", [C, B * N], F32).ap()
    x1 = nc.dram_tensor("x1", [C, B * N], F32).ap()
    ao1 = nc.dram_tensor("ao1", [C, B * N], F32).ap()
    ctx = ExitStack()
    with ctx:
        xs = ctx.enter_context(nc.sbuf_tensor("xs", [P, KC, B, N], F32))
        cst = constants(nc, ctx)
        attention_top(nc, cst, xs, t["x"], t["w_q0"], t["w_k0"], t["w_v0"], t["b_q"], t["b_k"], t["b_v"], ao0)
        mlp(nc, cst, xs, ao0, x1, t["w_o"], t["b_o"], t["w_1"], t["b_1"], t["g_1"], t["be_1"],
            t["w_2"], t["b_2"], t["g_2"], t["be_2"], t["g_rms"])
        attention_full(nc, cst, xs, t["w_q1"], t["w_k1"], t["w_v1"], ao1)
        output(nc, xs, ao1, x1, t["w_out"], t["b_out"], out)


def per_head(w):
    return np.ascontiguousarray(w.reshape(HEADS, D, KC, P).transpose(0, 3, 2, 1))


def per_partition(v, rows=P):
    return np.ascontiguousarray(v.reshape(-1, rows).T)


def kernel(**inputs):
    from concourse import bacc
    from concourse.bass_utils import run_bass_kernel_spmd

    a = {name: np.asarray(v) for name, v in inputs.items()}
    layer0 = {name[len("L0_conv_"):]: v for name, v in a.items() if name.startswith("L0_conv_")}
    qkv = a["L1_conv_w_qkv"]
    arrays = {
        "x": a["x"].reshape(B, C, N),
        "w_q0": per_head(layer0["Wq"]), "w_k0": per_head(layer0["Wk"]), "w_v0": per_head(layer0["Wv"]),
        "b_q": per_partition(layer0["bq"], D), "b_k": per_partition(layer0["bk"], D),
        "b_v": per_partition(layer0["bv"], D),
        "w_o": layer0["Wo"].T, "b_o": per_partition(layer0["bo"]),
        "w_1": layer0["W1"].T, "b_1": per_partition(layer0["b1"]),
        "g_1": per_partition(layer0["g1"]), "be_1": per_partition(layer0["be1"]),
        "w_2": layer0["W2"].T, "b_2": per_partition(layer0["b2"]),
        "g_2": per_partition(layer0["g2"]), "be_2": per_partition(layer0["be2"]),
        "g_rms": per_partition(a["L1_conv_g"]),
        "w_q1": per_head(qkv[0:C]), "w_k1": per_head(qkv[C:2 * C]), "w_v1": per_head(qkv[2 * C:3 * C]),
        "w_out": a["L1_conv_w_out"].T, "b_out": per_partition(a["L1_conv_b_out"]),
    }
    arrays = {name: np.ascontiguousarray(v) for name, v in arrays.items()}
    nc = bacc.Bacc("TRN2", target_bir_lowering=False, num_devices=1)
    t = {name: nc.dram_tensor(name, v.shape, F32, kind="ExternalInput").ap() for name, v in arrays.items()}
    out = nc.dram_tensor("out", [B, C, N], F32, kind="ExternalOutput").ap()
    build(nc, t, out)
    result = run_bass_kernel_spmd(nc, [arrays], core_ids=[0])
    return result.results[0]["out"].reshape(B, C, 48, 48)
```

```python
from contextlib import ExitStack

import numpy as np
import concourse.bass as bass
from concourse import mybir

F32 = mybir.dt.float32
F32R = mybir.dt.float32r
I32 = mybir.dt.int32
ALU = mybir.AluOpType
ACT = mybir.ActivationFunctionType
AX = mybir.AxisListType

P = 128
B, C, N = 2, 256, 48 * 48
KC = C // P
HEADS, D = 8, 32
MLP = 1024
MT = MLP // P
TOPK = 64
BN_EPS = 1e-5
SCALE = float(D) ** -0.5
BANK = 512

PAIR = 2 * P
PAIRS = N // PAIR
MCH = N // P
PRE = 6
PCOLS = N // PRE
PM = PCOLS // P
HEAD_STEPS = B * HEADS
ALL_PAIRS = HEAD_STEPS * PAIRS

CHUNK = 36
CHUNKS = N // CHUNK
KEEP = 3
CAND = CHUNKS * KEEP + 8
ROUNDS = TOPK // 8
LOWEST = -3.0e38
STEEP = 2.0 ** 60

SCOLS = [(c, min(BANK, N - c)) for c in range(0, N, BANK)]
TGROUPS = [(m, min(4, MCH - m)) for m in range(0, MCH, 4)]
NTG = len(TGROUPS)


def cols(start, n):
    return slice(start, start + n) if isinstance(start, int) else bass.ds(start, n)


class Tally:
    semaphore = None


def wait_alone(engine, semaphore, value):
    engine.wait_ge(semaphore, value)
    engine.sem_inc(Tally.semaphore, 1)


def constants(nc, ctx):
    sb = lambda name, shape, dt=F32: ctx.enter_context(nc.sbuf_tensor(name, shape, dt))
    k = {
        "ident": sb("ident", [P, P]),
        "ones": sb("ones", [P, P]),
        "ones_r": sb("ones_r", [P, P], F32R),
        "add_up": sb("add_up", [P, D]),
        "k_low": sb("k_low", [P, 1]),
        "q_low": sb("q_low", [P, 1]),
    }
    made = ctx.enter_context(nc.semaphore("constants_made"))
    Tally.semaphore = ctx.enter_context(nc.semaphore("waits_alone"))
    with nc.Block() as block:

        @block.gpsimd
        def _(pool):
            pool.memset(k["ident"][:, :], 0.0).then_inc(made, 1)
            pool.wait_ge(made, 1)
            pool.affine_select(out=k["ident"][:, :], in_=k["ident"][:, :], compare_op=ALU.not_equal,
                               fill=1.0, base=0, pattern=[[-1, P]],
                               channel_multiplier=1).then_inc(made, 1)

        @block.vector
        def _(dve):
            dve.memset(k["ones"][:, :], 1.0)
            dve.memset(k["ones_r"][:, :].bitcast(F32), 1.0)
            for quadrant in range(4):
                rows = slice(D * quadrant, D * quadrant + D)
                dve.memset(k["k_low"][rows, :], float(quadrant >= 2))
                dve.memset(k["q_low"][rows, :], float(quadrant % 2))
            dve.wait_ge(made, 2)
            for quadrant in range(4):
                rows = slice(D * quadrant, D * quadrant + D)
                dve.tensor_copy(k["add_up"][rows, :], k["ident"][rows, rows])
    return k


def over_steps(engine, step):
    with engine.Fori(0, HEADS) as h:
        for b in range(B):
            head = h * B + b
            with engine.Fori(0, PRE // 2) as half:
                for r in range(2):
                    step(head * PAIRS + half * 2 + r, half * 2 + r, (b + r) % 2, h, b, head)
            for i in range(PRE, PAIRS):
                step(head * PAIRS + i, i, (b + i) % 2, h, b, head)


class BankUses:

    def __init__(self, plain, preparing, before):
        self.plain, self.preparing, self.before = plain, preparing, before
        self.head = PRE * preparing + (PAIRS - PRE) * plain

    def __call__(self, head, i):
        if isinstance(i, int) and i >= PRE:
            return head * self.head + self.before + PRE * self.preparing + (i - PRE) * self.plain
        return head * self.head + self.before + i * self.preparing


def load_projections(sync, w_s, drams, h, loaded):
    for t, w in zip(w_s, drams):
        for r in range(t.shape[2] // D):
            sync.dma_start(t[:, :, D * r:D * r + D], w[h]).then_inc(loaded, 16)


class Shared:

    def __init__(self, nc, ctx, cst, xs, name, ahead, uses):
        sb = lambda n, shape, dt=F32: ctx.enter_context(nc.sbuf_tensor(name + n, shape, dt))
        sem = lambda n: ctx.enter_context(nc.semaphore(name + n))
        self.cst, self.xs, self.uses = cst, xs, uses
        self.ahead = ahead
        self.wq_s, self.wk_s, self.wv_s = sb("wq", [P, KC, 4 * D]), sb("wk", [P, KC, 4 * D]), sb("wv", [P, KC, D])
        self.bq_s, self.bk_s, self.bv_s = sb("bq", [P, HEADS + 1]), sb("bk", [P, HEADS + 1]), sb("bv", [D, HEADS + 1])
        self.k_raw, self.k_part = sb("k_raw", [P, PCOLS]), sb("k_part", [P, PCOLS], F32R)
        self.q_raw, self.q_part = sb("q_raw", [P, PAIR]), sb("q_part", [P, PAIR], F32R)
        self.k_stack = [sb(f"k_stack{n}", [P, N], F32R) for n in range(2)]
        self.q_stack = [sb(f"q_stack{n}", [P, PAIR], F32R) for n in range(2)]
        self.v_cols = sb("v_cols", [D, PCOLS])
        self.o_head = [sb(f"o_head{n}", [D, N]) for n in range(2)]
        self.bank = ctx.enter_context(nc.psum_tensor(name + "bank", [P, BANK], F32))
        self.x_loaded, self.bias_loaded = sem("x_loaded"), sem("bias_loaded")
        self.wq_loaded, self.wkv_loaded = sem("wq_loaded"), sem("wkv_loaded")
        self.buffers_set = sem("buffers_set")
        self.bank_filled, self.bank_kept = sem("bank_filled"), sem("bank_kept")
        self.k_stack_ready, self.q_stack_ready = sem("k_stack_ready"), sem("q_stack_ready")
        self.o_ready, self.o_stored = sem("o_ready"), sem("o_stored")
        self.pool_order = sem("pool_order")

    def load_first(self, sync, w_q, w_k, w_v, biases):
        load_projections(sync, (self.wk_s, self.wv_s), (w_k, w_v), 0, self.wkv_loaded)
        load_projections(sync, (self.wq_s,), (w_q,), 0, self.wq_loaded)
        if biases:
            sync.wait_ge(self.buffers_set, 1)
            for t, src in zip((self.bq_s, self.bk_s, self.bv_s), biases):
                for r in range(t.shape[0] // D):
                    sync.dma_start(t[D * r:D * r + D, 0:HEADS],
                                   src).then_inc(self.bias_loaded, 16)

    def load_and_store(self, sync, w_q, w_k, w_v, ao, wait_written):
        sync.sem_inc(self.o_stored, 32)

        def store(h, b):
            wait_written(h * B + b)
            sync.dma_start(ao.rearrange("(h d) n -> h d n", d=D)[h, :, b * N:b * N + N],
                           self.o_head[b][:, :]).then_inc(self.o_stored, 16)

        def per_head(h, h_next):
            sync.wait_ge(self.bank_filled, self.uses(h * B, PRE))
            load_projections(sync, (self.wk_s, self.wv_s), (w_k, w_v), h_next, self.wkv_loaded)
            store(h, 0)
            sync.wait_ge(self.bank_filled, self.uses(h * B + 1, PAIRS - self.ahead - 1) + 1)
            load_projections(sync, (self.wq_s,), (w_q,), h_next, self.wq_loaded)
            store(h, 1)

        with sync.Fori(0, HEADS - 1) as h:
            per_head(h, h + 1)
        per_head(HEADS - 1, HEADS - 1)
        sync.wait_ge(self.o_stored, 32 + 16 * HEAD_STEPS)

    def bank_free(self, pe, use):
        if not (isinstance(use, int) and use == 0):
            wait_alone(pe, self.bank_kept, use)

    def project(self, pe, use, out, weights, b, col, n):
        self.bank_free(pe, use)
        for kc in range(KC):
            last = pe.matmul(out, weights[:, kc, :], self.xs[:, kc, b, cols(col, n)],
                             start=kc == 0, stop=kc == KC - 1)
        last.then_inc(self.bank_filled, 1)

    def project_q(self, pe, use, b, i):
        self.project(pe, use, self.bank[:, 0:PAIR], self.wq_s, b, i * PAIR, PAIR)

    def project_k(self, pe, use, b, c):
        self.project(pe, use, self.bank[:, 0:PCOLS], self.wk_s, b, c * PCOLS, PCOLS)

    def project_v(self, pe, use, b, c):
        self.project(pe, use, self.bank[0:D, 0:PCOLS], self.wv_s, b, c * PCOLS, PCOLS)

    def turn_v(self, pe, use):
        self.bank_free(pe, use)
        for m in range(PM):
            last = pe.transpose(self.bank[:, D * m:D * m + D], self.v_cols[:, P * m:P * m + P],
                                self.cst["ident"][0:D, 0:D])
        last.then_inc(self.bank_filled, 1)

    def keep(self, act, use, out, rows, n, bias):
        wait_alone(act, self.bank_filled, use + 1)
        act.activation(out, self.bank[0:rows, 0:n], ACT.Identity, bias=bias).then_inc(self.bank_kept, 1)

    def keep_q(self, act, use, h, pairs_before):
        if not (isinstance(pairs_before, int) and pairs_before == 0):
            act.wait_ge(self.q_stack_ready, pairs_before)
        self.keep(act, use, self.q_raw[:, :], P, PAIR, self.bq_s[:, cols(h, 1)])

    def keep_k(self, act, use, h, chunks_before):
        if not (isinstance(chunks_before, int) and chunks_before == 0):
            act.wait_ge(self.k_stack_ready, chunks_before)
        self.keep(act, use, self.k_raw[:, :], P, PCOLS, self.bk_s[:, cols(h, 1)])

    def keep_v(self, act, use, h):
        self.keep(act, use, self.v_cols[:, :], D, PCOLS, self.bv_s[:, cols(h, 1)])

    def split(self, pool, raw, low, part, out, order, done):
        pool.tensor_scalar(part, raw, 0.0, low[:, 0:1], ALU.add, ALU.mult).then_inc(self.pool_order, 1)
        pool.wait_ge(self.pool_order, order)
        pool.tensor_tensor(out, raw, part.bitcast(F32), ALU.subtract).then_inc(done, 1)

    def split_k(self, pool, use, b, c, order):
        wait_alone(pool, self.bank_kept, use + 1)
        self.split(pool, self.k_raw[:, :], self.cst["k_low"], self.k_part[:, :],
                   self.k_stack[b][:, cols(c * PCOLS, PCOLS)], order, self.k_stack_ready)

    def split_q(self, pool, use, parity, order):
        wait_alone(pool, self.bank_kept, use + 1)
        self.split(pool, self.q_raw[:, :], self.cst["q_low"], self.q_part[:, :],
                   self.q_stack[parity][:, :], order, self.q_stack_ready)


def attention_top(nc, cst, xs, x, w_q, w_k, w_v, b_q, b_k, b_v, ao):
    ctx = ExitStack()
    with ctx:
        sb = lambda name, shape, dt=F32: ctx.enter_context(nc.sbuf_tensor("a_" + name, shape, dt))
        sem = lambda name: ctx.enter_context(nc.semaphore("a_" + name))
        uses = BankUses(plain=3, preparing=4, before=PRE + 3)
        sh = Shared(nc, ctx, cst, xs, "a_", 3, uses)
        v_s = [sb(f"v{n}", [P, MCH, D]) for n in range(2)]
        scores = [sb(f"scores{n}", [P, N]) for n in range(4)]
        probs = [sb(f"probs{n}", [P, N]) for n in range(2)]
        probs_t = [sb(f"probs_t{n}", [P, MCH, P]) for n in range(2)]
        scratch = sb("scratch", [P, N])
        top8 = sb("top8", [P, 2, CHUNKS + 1, 8])
        cand = sb("cand", [P, 2, CAND])
        best = sb("best", [P, 2, TOPK])
        missed = sb("missed", [P, 2])
        flag, flag_t, flags = sb("flag", [P, D]), sb("flag_t", [P, D]), sb("flags", [1, P])
        any_missed = sb("any_missed", [1, 1], I32)
        steep_kth = [sb(f"steep_kth{n}", [P, 2]) for n in range(2)]
        minus_max = [sb(f"minus_max{n}", [P, 2]) for n in range(2)]
        above = sb("above", [P, 2])
        sums, one_by_sum = sb("sums", [P, 2]), sb("one_by_sum", [P, 2])
        diagonal = [sb(f"diagonal{n}", [P, P]) for n in range(2)]
        parts = sb("parts", [P, PAIR])

        ps_s = ctx.enter_context(nc.psum_tensor("a_ps_s", [P, 5 * BANK], F32))
        ps_t = [ctx.enter_context(nc.psum_tensor(f"a_ps_t{n}", [P, BANK], F32)) for n in range(2)]

        scores_done, scores_kept = sem("scores_done"), sem("scores_kept")
        kth_ready = sem("kth_ready")
        penalty_ready, masked_ready, probs_ready = sem("penalty_ready"), sem("masked_ready"), sem("probs_ready")
        turned, turned_kept = sem("turned"), sem("turned_kept")
        diagonal_ready = sem("diagonal_ready")
        v_projected, v_cols_kept, v_turned, v_kept = (sem("v_projected"), sem("v_cols_kept"), sem("v_turned"),
                                                      sem("v_kept"))
        tops_taken, dve_order = sem("tops_taken"), sem("dve_order")

        block = ctx.enter_context(nc.Block())

        @block.sync
        def _(sync):
            for b in range(B):
                for kc in range(KC):
                    sync.dma_start(xs[:, kc, b, :], x[b, kc * P:kc * P + P, :]).then_inc(sh.x_loaded, 16)
            sh.load_first(sync, w_q, w_k, w_v, (b_q, b_k, b_v))
            sh.load_and_store(sync, w_q, w_k, w_v, ao,
                              lambda head: sync.wait_ge(sh.bank_kept, uses(head, PAIRS)))

        @block.tensor
        def _(pe):
            def score(tile, u, parity, b, first=False):
                if not first:
                    pe.wait_ge(scores_kept, tile)
                for c, n in SCOLS:
                    last = pe.matmul(ps_s[:, c:c + n], sh.q_stack[parity][:, P * u:P * u + P],
                                     sh.k_stack[b][:, c:c + n], start=True, stop=True)
                last.then_inc(scores_done, 1)

            def turn(u, g):
                m0, n = TGROUPS[g]
                bank = ps_t[(NTG * u + g) % 2]
                for m in range(n):
                    last = pe.matmul(bank[:, P * m:P * m + P], probs[u][:, P * (m0 + m):P * (m0 + m) + P],
                                     diagonal[u][:, :], start=True, stop=True)
                last.then_inc(turned, 1)

            def weigh(tile, u, g, b):
                pe.wait_ge(turned_kept, tile * NTG + g + 1)
                m0, n = TGROUPS[g]
                for m in range(m0, m0 + n):
                    rows = slice(D * (m % 4), D * (m % 4) + D)
                    last = pe.matmul(sh.bank[rows, P * u:P * u + P], v_s[b][:, m, :], probs_t[u][:, m, :],
                                     start=m < 4, stop=m + 4 >= MCH)
                return last

            pe.wait_ge(sh.x_loaded, 16 * B * KC)
            def project_v(b, c):
                for kc in range(KC):
                    last = pe.matmul(ps_t[0][0:D, 0:PCOLS], sh.wv_s[:, kc, :], xs[:, kc, b, cols(c * PCOLS, PCOLS)],
                                     start=kc == 0, stop=kc == KC - 1)
                last.then_inc(v_projected, 1)

            def turn_v(n):
                wait_alone(pe, v_cols_kept, n + 1)
                for m in range(PM):
                    last = pe.transpose(ps_t[1][:, D * m:D * m + D], sh.v_cols[:, P * m:P * m + P],
                                        cst["ident"][0:D, 0:D])
                last.then_inc(v_turned, 1)

            pe.wait_ge(sh.wkv_loaded, 80)
            for c in range(PRE):
                project_v(0, c)
                sh.project_k(pe, c, 0, c)
                turn_v(c)
                pe.wait_ge(v_kept, c + 1)
            pe.wait_ge(sh.wq_loaded, 64)
            for n in range(3):
                sh.project_q(pe, PRE + n, 0, n)
            pe.wait_ge(sh.k_stack_ready, PRE)
            for n in range(2):
                pe.wait_ge(sh.q_stack_ready, n + 1)
                for u in range(2):
                    score(2 * n + u, u, n, 0, first=n + u == 0)
            pe.wait_ge(sh.q_stack_ready, 3)
            score(4, 0, 0, 0)

            def step(pair, i, parity, h, b, head):
                use = uses(head, i)
                tail = isinstance(i, int)
                if tail and i + 3 == PAIRS:
                    pe.wait_ge(sh.wq_loaded, 64 * (h + b + 1))
                if tail and i + 3 >= PAIRS:
                    sh.project_q(pe, use, 1 - b, i + 3 - PAIRS)
                else:
                    sh.project_q(pe, use, b, i + 3)
                if not tail:
                    chunk = (head + 1) * PRE + i
                    wait_alone(pe, sh.wkv_loaded, 80 * (h + b + 1))
                    project_v(1 - b, i)
                    sh.project_k(pe, use + 1, 1 - b, i)
                    turn_v(chunk)
                use = use + (1 if tail else 2)
                pe.wait_ge(diagonal_ready, 2 * pair + 1)
                turn(0, 0)
                if not tail:
                    pe.wait_ge(v_kept, chunk + 1)
                turn(0, 1)
                score(2 * pair + 5, 1, parity, 1 - b if tail and i + 2 >= PAIRS else b)
                sh.bank_free(pe, use)
                for g in range(NTG):
                    weigh(2 * pair, 0, g, b)
                    if g + 2 < NTG:
                        turn(0, g + 2)
                    if g == 3:
                        if tail and i + 3 == PAIRS:
                            pe.wait_ge(sh.k_stack_ready, (head + 2) * PRE)
                        pe.wait_ge(sh.q_stack_ready, pair + 4)
                        score(2 * pair + 6, 0, 1 - parity, 1 - b if tail and i + 3 >= PAIRS else b)
                        pe.wait_ge(diagonal_ready, 2 * pair + 2)
                        turn(1, 0)
                turn(1, 1)
                for g in range(NTG):
                    last = weigh(2 * pair + 1, 1, g, b)
                    if g + 2 < NTG:
                        turn(1, g + 2)
                last.then_inc(sh.bank_filled, 1)
                sh.bank_free(pe, use + 1)
                pe.matmul(sh.bank[0:D, 0:PAIR], cst["add_up"][:, :], parts[:, :], start=True,
                          stop=True).then_inc(sh.bank_filled, 1)

            over_steps(pe, step)

        @block.scalar
        def _(act):
            def keep_v_cols(h, n):
                wait_alone(act, v_projected, n + 1)
                act.activation(sh.v_cols[:, :], ps_t[0][0:D, 0:PCOLS], ACT.Identity,
                               bias=sh.bv_s[:, cols(h, 1)]).then_inc(v_cols_kept, 1)

            def keep_v(b, c, n):
                wait_alone(act, v_turned, n + 1)
                act.activation(v_s[b][:, cols(c * PM, PM), :],
                               ps_t[1][:, 0:PM * D].rearrange("p (m d) -> p m d", d=D),
                               ACT.Copy).then_inc(v_kept, 1)

            def keep_scores(tile, n):
                act.wait_ge(scores_done, tile + 1)
                act.activation(scores[n][:, :], ps_s[:, 0:N], ACT.Copy).then_inc(scores_kept, 1)

            act.wait_ge(sh.bias_loaded, 16 * 9)
            for c in range(PRE):
                keep_v_cols(0, c)
                sh.keep_k(act, c, 0, c)
                keep_v(0, c, c)
            for n in range(3):
                sh.keep_q(act, PRE + n, 0, n)
            for n in range(4):
                keep_scores(n, n)

            def exponentials(tile, u, parity):
                act.wait_ge(masked_ready, tile + 1)
                act.activation(probs[u][:, :], probs[u][:, :], ACT.Exp, scale=SCALE,
                               bias=minus_max[parity][:, u:u + 1], accum_out=sums[:, u:u + 1]
                               ).then_inc(probs_ready, 1)

            def keep_turned(tile, u, g):
                m0, n = TGROUPS[g]
                act.wait_ge(turned, tile * NTG + g + 1)
                act.activation(probs_t[u][:, m0:m0 + n, :],
                               ps_t[(NTG * u + g) % 2][:, 0:n * P].rearrange("p (m q) -> p m q", q=P),
                               ACT.Copy).then_inc(turned_kept, 1)

            def penalty(u, parity):
                act.activation(probs[u][:, :], scores[2 * parity + u][:, :], ACT.Relu, scale=-STEEP,
                               bias=steep_kth[parity][:, u:u + 1]).then_inc(penalty_ready, 1)

            act.wait_ge(kth_ready, 1)
            for u in range(2):
                penalty(u, 0)

            def step(pair, i, parity, h, b, head):
                use = uses(head, i)
                tail = isinstance(i, int)
                chunk = (head + 1) * PRE + i
                exponentials(2 * pair, 0, parity)
                sh.keep_q(act, use, h + b if tail and i + 3 >= PAIRS else h, pair + 3)
                if not tail:
                    keep_v_cols(h + b, chunk)
                keep_scores(2 * pair + 4, 2 * parity)
                if not tail:
                    sh.keep_k(act, use + 1, h + b, chunk)
                    keep_v(1 - b, i, chunk)
                use = use + (1 if tail else 2)
                for g in range(2):
                    keep_turned(2 * pair, 0, g)
                exponentials(2 * pair + 1, 1, parity)
                keep_turned(2 * pair, 0, 2)
                keep_scores(2 * pair + 5, 2 * parity + 1)
                for g in range(3, NTG):
                    keep_turned(2 * pair, 0, g)
                keep_turned(2 * pair + 1, 1, 0)
                act.wait_ge(kth_ready, pair + 2)
                penalty(0, 1 - parity)
                for g in range(1, NTG):
                    keep_turned(2 * pair + 1, 1, g)
                act.wait_ge(sh.bank_filled, use + 1)
                act.activation(parts[:, :], sh.bank[:, 0:PAIR], ACT.Copy).then_inc(sh.bank_kept, 1)
                penalty(1, 1 - parity)
                wait_alone(act, sh.o_stored, 16 * (head + 1))
                wait_alone(act, sh.bank_filled, use + 2)
                act.activation(sh.o_head[b][:, cols(i * PAIR, PAIR)], sh.bank[0:D, 0:PAIR],
                               ACT.Copy).then_inc(sh.bank_kept, 1)

            over_steps(act, step)

        @block.gpsimd
        def _(pool):
            for c in range(PRE):
                sh.split_k(pool, c, 0, c, c + 1)
            for n in range(3):
                if n == 2:
                    pool.wait_ge(scores_done, 2)
                sh.split_q(pool, PRE + n, n % 2, PRE + n + 1)

            def step(pair, i, parity, h, b, head):
                use = uses(head, i)
                tail = isinstance(i, int)
                splits = PRE + 3 + head * (PAIRS + PRE) + (PRE + i if tail else i * 2)
                for u in range(2):
                    pool.wait_ge(penalty_ready, 2 * pair + u + 1)
                    pool.tensor_tensor(probs[u][:, :], scores[2 * parity + u][:, :], probs[u][:, :],
                                       ALU.subtract).then_inc(masked_ready, 1)
                pool.wait_ge(scores_done, 2 * pair + 4)
                sh.split_q(pool, use, 1 - parity, splits + 1)
                if not tail:
                    sh.split_k(pool, use + 1, 1 - b, i, splits + 2)

            over_steps(pool, step)

        @block.vector
        def _(dve):
            at = {"n": 0}

            def counted(instruction):
                at["n"] += 1
                instruction.then_inc(dve_order, 1)
                return at["n"]

            def chunk_tops(pair, parity, u, between=lambda c: None):
                wait_alone(dve, scores_kept, 2 * pair + u + 1)
                for c in range(CHUNKS):
                    last = dve.max(top8[:, u, c, :], scores[2 * parity + u][:, CHUNK * c:CHUNK * c + CHUNK])
                    if c < CHUNKS - 1:
                        between(c)
                last.then_inc(tops_taken, 1)

            def one_by_sums(pair, u):
                wait_alone(dve, probs_ready, 2 * pair + u + 1)
                return counted(dve.reciprocal(one_by_sum[:, u:u + 1], sums[:, u:u + 1]))

            def diagonals(u):
                dve.tensor_scalar(diagonal[u][:, :], cst["ident"][:, :], one_by_sum[:, u:u + 1], None,
                                  ALU.mult).then_inc(diagonal_ready, 1)

            def select(pair):
                at["n"] = 0
                after = lambda n: dve.wait_ge(dve_order, n)
                wait_alone(dve, tops_taken, 2 * pair + 2)
                rest, written = [0, 0], [0, 0]
                for u in range(2):
                    rest[u] = counted(dve.max(top8[:, u, CHUNKS, :], top8[:, u, 0:CHUNKS, KEEP:8]))
                    counted(dve.tensor_copy(cand[:, u, 0:CHUNKS * KEEP].rearrange("p (c k) -> p c k", k=KEEP),
                                            top8[:, u, 0:CHUNKS, 0:KEEP]))
                for u in range(2):
                    after(rest[u])
                    written[u] = counted(dve.tensor_copy(cand[:, u, CHUNKS * KEEP:CAND], top8[:, u, CHUNKS, :]))
                counted(dve.tensor_reduce(missed[:, :], top8[:, :, :, 7], AX.X, ALU.max))
                for r in range(ROUNDS):
                    found = [0, 0]
                    for u in range(2):
                        after(written[u])
                        found[u] = counted(dve.max(best[:, u, 8 * r:8 * r + 8], cand[:, u, :]))
                    previous = not (isinstance(pair, int) and pair == 0)
                    if previous and r == 3:
                        summed = one_by_sums(pair - 1, 0)
                    if r < ROUNDS - 1:
                        for u in range(2):
                            after(found[u])
                            written[u] = counted(dve.match_replace(cand[:, u, :], best[:, u, 8 * r:8 * r + 8],
                                                                   cand[:, u, :], LOWEST))
                    if previous and r == 3:
                        after(summed)
                        diagonals(0)

            def any_of(marks, stage):
                if stage == 0:
                    return dve.tensor_reduce(flag[:, 0:1], marks[:, :], AX.X, ALU.max)
                if stage == 1:
                    return dve.transpose(flag_t[:, :], flag[:, :])
                if stage == 2:
                    for q in range(4):
                        last = dve.tensor_copy(flags[:, D * q:D * q + D], flag_t[D * q:D * q + 1, :])
                    return last
                return dve.tensor_reduce(any_missed[:, :], flags[:, :], AX.X, ALU.max)

            def check(c):
                if c in (1, 3, 5, 7, 9):
                    dve.wait_ge(dve_order, at["n"])
                    if c == 1:
                        counted(dve.tensor_tensor(missed[:, :], missed[:, :], best[:, :, TOPK - 1], ALU.is_gt))
                    else:
                        counted(any_of(missed, (c - 3) // 2))

            def hand_on(pair, parity):
                dve.wait_ge(dve_order, at["n"])
                doubtful = dve.value_load(any_missed[0:1, 0:1], min_val=0, max_val=1)
                dve.sem_clear(dve_order)
                with dve.If(doubtful > 0):
                    for u in range(2):
                        dve.tensor_scalar(scratch[:, :], scores[2 * parity + u][:, :],
                                          best[:, u, TOPK - 1:TOPK], None, ALU.is_gt, ALU.add,
                                          accum_out=above[:, u:u + 1])
                        dve.drain()
                    dve.tensor_scalar(above[:, :], above[:, :], TOPK - 0.5, None, ALU.is_gt)
                    for stage in range(4):
                        dve.drain()
                        any_of(above, stage)
                    dve.drain()
                    again = dve.value_load(any_missed[0:1, 0:1], min_val=0, max_val=1)
                    with dve.If(again > 0):
                        for u in range(2):
                            dve.tensor_copy(scratch[:, :], scores[2 * parity + u][:, :])
                            for r in range(ROUNDS):
                                dve.drain()
                                dve.max(best[:, u, 8 * r:8 * r + 8], scratch[:, :])
                                dve.drain()
                                if r < ROUNDS - 1:
                                    dve.match_replace(scratch[:, :], best[:, u, 8 * r:8 * r + 8], scratch[:, :],
                                                      LOWEST)
                dve.tensor_scalar(steep_kth[parity][:, :], best[:, :, TOPK - 1], STEEP, None, ALU.mult)
                dve.tensor_scalar(minus_max[parity][:, :], best[:, :, 0], -SCALE, None,
                                  ALU.mult).then_inc(kth_ready, 1)

            def pair_step(pair, parity):
                chunk_tops(pair, parity, 1)
                select(pair)

                def between(c):
                    check(c)
                    if not (isinstance(pair, int) and pair == 0):
                        if c == 24:
                            one_by_sums(pair - 1, 1)
                        if c == 26:
                            dve.wait_ge(dve_order, at["n"])
                            diagonals(1)

                chunk_tops(pair + 1, 1 - parity, 0, between)
                hand_on(pair, parity)

            for t in (sh.bq_s, sh.bk_s, sh.bv_s, flag):
                last = dve.memset(t[:, :], 0.0)
            last.then_inc(sh.buffers_set, 1)
            dve.wait_ge(sh.buffers_set, 1)
            chunk_tops(0, 0, 0)
            pair_step(0, 0)
            with dve.Fori(0, (ALL_PAIRS - 2) // 2) as k:
                pair_step(k * 2 + 1, 1)
                pair_step(k * 2 + 2, 0)
            pair_step(ALL_PAIRS - 1, 1)
            at["n"] = 0
            for u in range(2):
                dve.wait_ge(dve_order, one_by_sums(ALL_PAIRS - 1, u))
                diagonals(u)
            dve.sem_inc(kth_ready, 1)


def mlp(nc, cst, xs, ao, x1, w_o, b_o, w_1, b_1, g_1, be_1, w_2, b_2, g_2, be_2, g_rms):
    CW = BANK
    NCH = B * N // CW
    ctx = ExitStack()
    with ctx:
        sb = lambda name, shape, dt=F32: ctx.enter_context(nc.sbuf_tensor("m_" + name, shape, dt))
        sem = lambda name: ctx.enter_context(nc.semaphore("m_" + name))
        hid = sb("hid", [P, NCH, MT, CW])
        w = sb("w", [P, KC * MLP])
        w1_s = w[:, :].rearrange("p (k m) -> p k m", k=KC)
        w2_s = w[:, :].rearrange("p (k c) -> p k c", k=MT)
        wo_s = sb("wo", [P, KC, C])
        vec = {n: sb(n, [P, m]) for n, m in (("b_o", KC), ("b_1", MT), ("g_1", MT), ("be_1", MT), ("b_2", KC),
                                             ("g_2", KC), ("be_2", KC), ("g_rms", KC))}
        stats1, mean1 = sb("stats1", [P, MT, NCH * 6]), sb("mean1", [P, MT, 2])
        stats2, mean2 = sb("stats2", [P, KC, NCH * 6]), sb("mean2", [P, KC, 2])
        scale1, shift1 = sb("scale1", [P, MT]), sb("shift1", [P, MT])
        scale2, shift2 = sb("scale2", [P, KC]), sb("shift2", [P, KC])
        ps_o = ctx.enter_context(nc.psum_tensor("m_ps_o", [P, KC, BANK], F32))
        ps_h = [ctx.enter_context(nc.psum_tensor(f"m_ps_h{n}", [P, BANK], F32)) for n in range(4)]
        xf = xs[:, :, :, :].rearrange("p k b n -> p k (b n)")

        first_ao_loaded, ao_loaded = sem("first_ao_loaded"), sem("ao_loaded")
        w1_loaded, w2_loaded, vec_loaded = sem("w1_loaded"), sem("w2_loaded"), sem("vec_loaded")
        proj_done, o_ready = sem("proj_done"), sem("o_ready")
        hid_done, hid_kept = sem("hid_done"), sem("hid_kept")
        var1_ready, dev1_ready, bn1_ready, bn_order = (sem("var1_ready"), sem("dev1_ready"), sem("bn1_ready"),
                                                       sem("bn_order"))
        relu_done, y_done, y_kept = sem("relu_done"), sem("y_done"), sem("y_kept")
        var2_ready, dev2_ready, bn2_ready = sem("var2_ready"), sem("dev2_ready"), sem("bn2_ready")
        y_scaled, x1_ready, x1_stored = sem("y_scaled"), sem("x1_ready"), sem("x1_stored")
        squares_ready, sums_done, norm_ready = sem("squares_ready"), sem("sums_done"), sem("norm_ready")
        xn_order, xn_ready = sem("xn_order"), sem("xn_ready")
        block = ctx.enter_context(nc.Block())

        def ao_slot(c, n):
            return hid[:, cols(c, n), MT - KC:MT, :]

        @block.sync
        def _(sync):
            sync.dma_start(wo_s[:, :, :], w_o.rearrange("(k p) o -> p k o", p=P)).then_inc(first_ao_loaded, 16)
            for kc in range(KC):
                src = ao[kc * P:kc * P + P, :].rearrange("p (c n) -> p c n", n=CW)
                sync.dma_start(hid[:, 0, MT - KC + kc, :], src[:, 0, :]).then_inc(first_ao_loaded, 16)
            for kc in range(KC):
                src = ao[kc * P:kc * P + P, :].rearrange("p (c n) -> p c n", n=CW)
                sync.dma_start(hid[:, 1:NCH, MT - KC + kc, :], src[:, 1:NCH, :]).then_inc(ao_loaded, 16)
            sync.dma_start(w1_s, w_1.rearrange("(k p) o -> p k o", p=P)).then_inc(w1_loaded, 16)
            for name, src in (("b_o", b_o), ("b_1", b_1), ("g_1", g_1), ("be_1", be_1), ("b_2", b_2),
                              ("g_2", g_2), ("be_2", be_2), ("g_rms", g_rms)):
                sync.dma_start(vec[name][:, :], src).then_inc(vec_loaded, 16)
            sync.wait_ge(hid_done, NCH * MT)
            sync.dma_start(w2_s, w_2.rearrange("(k p) o -> p k o", p=P)).then_inc(w2_loaded, 16)
            sync.wait_ge(x1_ready, NCH)
            for kc in range(KC):
                sync.dma_start(x1[kc * P:kc * P + P, :].rearrange("p (c n) -> p c n", n=CW),
                               hid[:, :, kc, :]).then_inc(x1_stored, 16)
            sync.wait_ge(x1_stored, 16 * KC)

        @block.tensor
        def _(pe):
            def project(c):
                pe.wait_ge(o_ready, c)
                for oc in range(KC):
                    for kc in range(KC):
                        last = pe.matmul(ps_o[:, oc, :], wo_s[:, kc, P * oc:P * oc + P],
                                         hid[:, c, MT - KC + kc, :], start=kc == 0, stop=kc == KC - 1)
                last.then_inc(proj_done, 1)

            def hidden(c):
                pe.wait_ge(o_ready, c + 1)
                for mt in range(MT):
                    pe.wait_ge(hid_kept, c * MT + mt + 1)
                    for kc in range(KC):
                        last = pe.matmul(ps_h[mt % 4][:, :], w1_s[:, kc, P * mt:P * mt + P],
                                         xf[:, kc, cols(c * CW, CW)], start=kc == 0, stop=kc == KC - 1)
                    last.then_inc(hid_done, 1)

            pe.wait_ge(first_ao_loaded, 16 * 3)
            for oc in range(KC):
                for kc in range(KC):
                    last = pe.matmul(ps_o[:, oc, :], wo_s[:, kc, P * oc:P * oc + P], hid[:, 0, MT - KC + kc, :],
                                     start=kc == 0, stop=kc == KC - 1)
            last.then_inc(proj_done, 1)
            pe.wait_ge(ao_loaded, 16 * KC)
            pe.wait_ge(w1_loaded, 16)
            with pe.Fori(0, NCH - 1) as c:
                project(c + 1)
                hidden(c)
            hidden(NCH - 1)

            pe.wait_ge(w2_loaded, 16)
            with pe.Fori(0, NCH) as c:
                for oc in range(KC):
                    pe.wait_ge(y_kept, c * KC + oc + 1)
                    for mt in range(MT):
                        if oc == 0:
                            pe.wait_ge(relu_done, c * MT + mt + 1)
                        last = pe.matmul(ps_o[:, oc, :], w2_s[:, mt, P * oc:P * oc + P], hid[:, c, mt, :],
                                         start=mt == 0, stop=mt == MT - 1)
                    last.then_inc(y_done, 1)

            with pe.Fori(0, NCH) as c:
                pe.wait_ge(squares_ready, c + 1)
                pe.wait_ge(norm_ready, c + 1)
                for kc in range(KC):
                    last = pe.matmul(ps_h[0][:, :], cst["ones"][:, :], hid[:, c, KC + kc, :],
                                     start=kc == 0, stop=kc == KC - 1)
                last.then_inc(sums_done, 1)

        @block.scalar
        def _(act):
            act.sem_inc(hid_kept, 4)
            act.sem_inc(y_kept, KC)
            act.sem_inc(norm_ready, 1)
            act.wait_ge(vec_loaded, 16 * 8)
            with act.Fori(0, NCH) as c:
                for mt in range(MT):
                    act.wait_ge(hid_done, c * MT + mt + 1)
                    act.activation(hid[:, c, mt, :], ps_h[mt % 4][:, :], ACT.Identity,
                                   bias=vec["b_1"][:, mt:mt + 1]).then_inc(hid_kept, 1)
            act.wait_ge(var1_ready, 1)
            act.activation(mean1[:, :, 1], mean1[:, :, 1], ACT.Sqrt).then_inc(dev1_ready, 1)
            act.wait_ge(bn1_ready, 1)

            def relu(c):
                for mt in range(MT):
                    act.activation(hid[:, c, mt, :], hid[:, c, mt, :], ACT.Relu, scale=scale1[:, mt:mt + 1],
                                   bias=shift1[:, mt:mt + 1]).then_inc(relu_done, 1)

            def keep_y(c):
                for oc in range(KC):
                    act.wait_ge(y_done, c * KC + KC)
                    act.activation(hid[:, c, oc, :], ps_o[:, oc, :], ACT.Identity,
                                   bias=vec["b_2"][:, oc:oc + 1]).then_inc(y_kept, 1)

            relu(0)
            with act.Fori(0, NCH - 1) as c:
                relu(c + 1)
                keep_y(c)
            keep_y(NCH - 1)
            act.wait_ge(var2_ready, 1)
            act.activation(mean2[:, :, 1], mean2[:, :, 1], ACT.Sqrt).then_inc(dev2_ready, 1)
            act.wait_ge(bn2_ready, 1)
            with act.Fori(0, NCH) as c:
                for kc in range(KC):
                    last = act.activation(hid[:, c, kc, :], hid[:, c, kc, :], ACT.Identity,
                                          scale=scale2[:, kc:kc + 1], bias=shift2[:, kc:kc + 1])
                last.then_inc(y_scaled, 1)
            with act.Fori(0, NCH) as c:
                act.wait_ge(x1_ready, c + 1)
                act.activation(hid[:, c, KC:2 * KC, :], hid[:, c, 0:KC, :], ACT.Square).then_inc(squares_ready, 1)
            with act.Fori(0, NCH) as c:
                act.wait_ge(sums_done, c + 1)
                act.activation(hid[:, c, 2 * KC, :], ps_h[0][:, :], ACT.Sqrt).then_inc(norm_ready, 1)

        @block.vector
        def _(dve):
            def residual(c):
                dve.wait_ge(proj_done, c + 1)
                for oc in range(KC):
                    x_c = xf[:, oc, cols(c * CW, CW)]
                    last = dve.scalar_tensor_tensor(x_c, ps_o[:, oc, :], vec["b_o"][:, oc:oc + 1], x_c,
                                                    ALU.add, ALU.add)
                last.then_inc(o_ready, 1)

            def hidden_stats(c):
                for mt in range(MT):
                    dve.wait_ge(hid_kept, c * MT + mt + 5)
                    last = dve.bn_stats(stats1[:, mt, cols(c * 6, 6)], hid[:, c, mt, :])
                return last

            def batchnorm(blocks, stats, mean, gamma, beta, scale, shift, var_ready, dev_ready, ready, order):
                for m in range(blocks):
                    last = dve.bn_aggr(mean[:, m, :], stats[:, m, :])
                last.then_inc(bn_order, 1)
                dve.wait_ge(bn_order, order + 1)
                dve.tensor_scalar(mean[:, :, 1], mean[:, :, 1], BN_EPS, None, ALU.add).then_inc(var_ready, 1)
                dve.wait_ge(dev_ready, 1)
                dve.reciprocal(scale[:, :], mean[:, :, 1]).then_inc(bn_order, 1)
                dve.wait_ge(bn_order, order + 2)
                dve.tensor_tensor(scale[:, :], scale[:, :], gamma[:, :], ALU.mult).then_inc(bn_order, 1)
                dve.wait_ge(bn_order, order + 3)
                dve.tensor_tensor(shift[:, :], mean[:, :, 0], scale[:, :], ALU.mult).then_inc(bn_order, 1)
                dve.wait_ge(bn_order, order + 4)
                dve.tensor_tensor(shift[:, :], beta[:, :], shift[:, :], ALU.subtract).then_inc(ready, 1)

            dve.wait_ge(vec_loaded, 16 * 8)
            residual(0)
            with dve.Fori(0, NCH - 1) as c:
                residual(c + 1)
                hidden_stats(c)
            hidden_stats(NCH - 1).then_inc(bn_order, 1)
            dve.wait_ge(bn_order, 1)
            batchnorm(MT, stats1, mean1, vec["g_1"], vec["be_1"], scale1, shift1, var1_ready, dev1_ready,
                      bn1_ready, 1)
            with dve.Fori(0, NCH) as c:
                for oc in range(KC):
                    dve.wait_ge(y_kept, c * KC + oc + 1 + KC)
                    dve.bn_stats(stats2[:, oc, cols(c * 6, 6)], hid[:, c, oc, :]).then_inc(xn_order, 1)
            dve.wait_ge(xn_order, NCH * KC)
            batchnorm(KC, stats2, mean2, vec["g_2"], vec["be_2"], scale2, shift2, var2_ready, dev2_ready,
                      bn2_ready, 5)
            with dve.Fori(0, NCH) as c:
                dve.wait_ge(y_scaled, c + 1)
                dve.tensor_tensor(hid[:, c, 0:KC, :], hid[:, c, 0:KC, :], xf[:, :, cols(c * CW, CW)],
                                  ALU.add).then_inc(x1_ready, 1)
            base = NCH * KC
            with dve.Fori(0, NCH) as c:
                norm = hid[:, c, 2 * KC, :]
                dve.wait_ge(norm_ready, c + 2)
                dve.tensor_scalar(norm, norm, 1e-12, None, ALU.max).then_inc(xn_order, 1)
                wait_alone(dve, xn_order, base + c * 2 + 1)
                dve.reciprocal(norm, norm).then_inc(xn_order, 1)
                dve.wait_ge(xn_order, base + c * 2 + 2)
                for kc in range(KC):
                    dve.scalar_tensor_tensor(xf[:, kc, cols(c * CW, CW)], hid[:, c, kc, :],
                                             vec["g_rms"][:, kc:kc + 1], norm, ALU.mult, ALU.mult)
            xn = xf[:, :, :]
            dve.drain()
            dve.tensor_scalar(xn, xn, float(C) ** 0.5, None, ALU.mult).then_inc(xn_ready, 1)
            dve.wait_ge(xn_ready, 1)


def attention_full(nc, cst, xs, w_q, w_k, w_v, ao):
    ctx = ExitStack()
    with ctx:
        sb = lambda name, shape, dt=F32: ctx.enter_context(nc.sbuf_tensor("b_" + name, shape, dt))
        sem = lambda name: ctx.enter_context(nc.semaphore("b_" + name))
        GROUPS, PER = MCH // 2, 2
        uses = BankUses(plain=2, preparing=5, before=3 * PRE + 2)
        sh = Shared(nc, ctx, cst, xs, "b_", 2, uses)
        v_raw = sb("v_raw", [P, PM, D])
        v_stack = [sb(f"v_stack{n}", [P, MCH, 3 * D], F32R) for n in range(2)]
        expo = [sb(f"expo{n}", [P, MCH, PAIR]) for n in range(2)]
        high, low = sb("high", [P, MCH, PAIR], F32R), sb("low", [P, MCH, PAIR], F32R)
        row_max = sb("row_max", [P, 2])
        minus_max = [sb(f"minus_max{n}", [P, PAIR], F32R) for n in range(2)]
        av_high, av_low, av_sum = sb("av_high", [D, PAIR]), sb("av_low", [D, PAIR]), sb("av_sum", [D, PAIR])
        rden = sb("rden", [D, PAIR])

        ps_s = ctx.enter_context(nc.psum_tensor("b_ps_s", [P, 5 * BANK], F32))
        ps_t = [ctx.enter_context(nc.psum_tensor(f"b_ps_t{n}", [P, PER, PAIR], F32)) for n in range(2)]

        scores_done, max_ready, diagonal_ready = sem("scores_done"), sem("max_ready"), sem("diagonal_ready")
        shifted_done, expo_ready = sem("shifted_done"), sem("expo_ready")
        high_ready, low_ready = sem("high_ready"), sem("low_ready")
        v_split = sem("v_split")
        rden_ready = sem("rden_ready")

        block = ctx.enter_context(nc.Block())

        @block.sync
        def _(sync):
            sh.load_first(sync, w_q, w_k, w_v, None)
            sh.load_and_store(sync, w_q, w_k, w_v, ao,
                              lambda head: sync.wait_ge(sh.o_ready, (head + 1) * PAIRS))

        @block.tensor
        def _(pe):
            def score(tile, u, parity, b, first=False):
                if not first:
                    pe.wait_ge(max_ready, tile)
                for c, n in SCOLS:
                    last = pe.matmul(ps_s[:, c:c + n], sh.q_stack[parity][:, P * u:P * u + P],
                                     sh.k_stack[b][:, c:c + n], start=True, stop=True)
                last.then_inc(scores_done, 1)

            def shifted(pair, g, parity, b):
                bank = ps_t[(parity + g) % 2]
                if g == 0:
                    pe.wait_ge(diagonal_ready, pair + 1)
                pe.wait_ge(expo_ready, pair * GROUPS + g + 1)
                for m in range(PER):
                    block_of_k = sh.k_stack[b][:, P * (PER * g + m):P * (PER * g + m) + P]
                    pe.matmul(bank[:, m, :], cst["ones_r"][:, :], minus_max[parity][:, :], start=True, stop=False)
                    last = pe.matmul(bank[:, m, :], block_of_k, sh.q_stack[parity][:, :], start=False, stop=True)
                last.then_inc(shifted_done, 1)

            def weigh(pair, g, b):
                pe.wait_ge(low_ready, pair * GROUPS + g + 1)
                for m in range(PER * g, PER * g + PER):
                    for part in (high, low):
                        last = pe.matmul(sh.bank[0:3 * D, 0:PAIR], v_stack[b][:, m, :], part[:, m, :],
                                         start=m == 0 and part is high, stop=m == MCH - 1 and part is low)
                return last

            pe.wait_ge(sh.wkv_loaded, 80)
            for c in range(PRE):
                sh.project_k(pe, 3 * c, 0, c)
                sh.project_v(pe, 3 * c + 1, 0, c)
                sh.turn_v(pe, 3 * c + 2)
            pe.wait_ge(sh.wq_loaded, 64)
            for n in range(2):
                sh.project_q(pe, 3 * PRE + n, 0, n)
            pe.wait_ge(sh.k_stack_ready, PRE)
            pe.wait_ge(sh.q_stack_ready, 1)
            for u in range(2):
                score(u, u, 0, 0, first=u == 0)
            for g in range(2):
                shifted(0, g, 0, 0)

            def step(pair, i, parity, h, b, head):
                use = uses(head, i)
                tail = isinstance(i, int)
                last_step = tail and i == PAIRS - 1
                next_b = 1 - b if last_step else b
                if tail and i + 2 == PAIRS:
                    pe.wait_ge(sh.wq_loaded, 64 * (h + b + 1))
                if tail and i + 2 >= PAIRS:
                    sh.project_q(pe, use, 1 - b, i + 2 - PAIRS)
                else:
                    sh.project_q(pe, use, b, i + 2)
                shifted(pair, 2, parity, b)
                if last_step:
                    pe.wait_ge(sh.k_stack_ready, (head + 2) * PRE)
                pe.wait_ge(sh.q_stack_ready, pair + 2)
                score(2 * pair + 2, 0, 1 - parity, next_b)
                shifted(pair, 3, parity, b)
                if not tail:
                    pe.wait_ge(sh.wkv_loaded, 80 * (h + b + 1))
                    sh.project_k(pe, use + 1, 1 - b, i)
                shifted(pair, 4, parity, b)
                if not tail:
                    sh.project_v(pe, use + 2, 1 - b, i)
                shifted(pair, 5, parity, b)
                if not tail:
                    sh.turn_v(pe, use + 3)
                score(2 * pair + 3, 1, 1 - parity, next_b)
                sh.bank_free(pe, use + 1 if tail else use + 4)
                pe.wait_ge(v_split, (head + 1) * PRE)
                weigh(pair, 0, b)
                for g in range(6, GROUPS):
                    shifted(pair, g, parity, b)
                    weigh(pair, 2 * g - 11, b)
                    weigh(pair, 2 * g - 10, b)
                for g in range(2):
                    shifted(pair + 1, g, 1 - parity, next_b)
                weigh(pair, 7, b)
                weigh(pair, 8, b).then_inc(sh.bank_filled, 1)

            over_steps(pe, step)

        @block.scalar
        def _(act):
            act.sem_inc(expo_ready, 2)

            def keep_turned_v(use, b, c):
                wait_alone(act, sh.bank_filled, use + 1)
                turned = sh.bank[:, 0:PM * D].rearrange("p (m d) -> p m d", d=D)
                act.activation(v_stack[b][:, cols(c * PM, PM), 0:D], turned, ACT.Copy)
                act.activation(v_raw[:, :, :], turned, ACT.Copy).then_inc(sh.bank_kept, 1)

            def exponentials(pair, g, parity):
                act.wait_ge(shifted_done, pair * GROUPS + g + 1)
                act.activation(expo[parity][:, PER * g:PER * g + PER, :], ps_t[(parity + g) % 2][:, :, :],
                               ACT.Exp, scale=SCALE).then_inc(expo_ready, 1)

            act.wait_ge(sh.buffers_set, 1)
            for c in range(PRE):
                sh.keep_k(act, 3 * c, 0, c)
                sh.keep_v(act, 3 * c + 1, 0)
                if c:
                    act.wait_ge(v_split, c)
                keep_turned_v(3 * c + 2, 0, c)
            for n in range(2):
                sh.keep_q(act, 3 * PRE + n, 0, n)
            for g in range(2):
                exponentials(0, g, 0)

            def step(pair, i, parity, h, b, head):
                use = uses(head, i)
                tail = isinstance(i, int)
                sh.keep_q(act, use, h + b if tail and i + 2 >= PAIRS else h, pair + 2)
                exponentials(pair, 2, parity)
                exponentials(pair, 3, parity)
                if not tail:
                    sh.keep_k(act, use + 1, h + b, (head + 1) * PRE + i)
                exponentials(pair, 4, parity)
                if not tail:
                    sh.keep_v(act, use + 2, h + b)
                exponentials(pair, 5, parity)
                if not tail:
                    act.wait_ge(v_split, (head + 1) * PRE + i)
                    keep_turned_v(use + 3, 1 - b, i)
                for g in range(6, GROUPS):
                    exponentials(pair, g, parity)
                for g in range(2):
                    exponentials(pair + 1, g, 1 - parity)
                act.wait_ge(sh.o_ready, pair)
                act.wait_ge(sh.bank_filled, (use + 1 if tail else use + 4) + 1)
                for n, t in enumerate((av_high, av_low, av_sum)):
                    last = act.activation(t[:, :], sh.bank[D * n:D * n + D, 0:PAIR], ACT.Copy)
                last.then_inc(sh.bank_kept, 1)

            over_steps(act, step)


        @block.gpsimd
        def _(pool):
            def split_v(use, b, c):
                wait_alone(pool, sh.bank_kept, use + 1)
                v_high = v_stack[b][:, cols(c * PM, PM), 0:D]
                pool.tensor_tensor(v_stack[b][:, cols(c * PM, PM), D:2 * D], v_raw[:, :, :],
                                   v_high.bitcast(F32), ALU.subtract).then_inc(v_split, 1)

            def low_part(pair, g, parity):
                pool.wait_ge(high_ready, pair * GROUPS + g + 1)
                blocks = slice(PER * g, PER * g + PER)
                pool.tensor_tensor(low[:, blocks, :], expo[parity][:, blocks, :], high[:, blocks, :].bitcast(F32),
                                   ALU.subtract).then_inc(low_ready, 1)

            for c in range(PRE):
                sh.split_k(pool, 3 * c, 0, c, c + 1)
                split_v(3 * c + 2, 0, c)
            for n in range(2):
                sh.split_q(pool, 3 * PRE + n, n, PRE + n + 1)

            def step(pair, i, parity, h, b, head):
                use = uses(head, i)
                tail = isinstance(i, int)
                order = PRE + 2 + head * (2 * PAIRS + PRE) + (PRE + i * 2 if tail else i * 3)
                for g in range(4):
                    low_part(pair, g, parity)
                if not tail:
                    sh.split_k(pool, use + 1, 1 - b, i, order + 1)
                for g in range(4, 6):
                    low_part(pair, g, parity)
                if not tail:
                    split_v(use + 3, 1 - b, i)
                    order = order + 1
                for g in range(6, GROUPS):
                    low_part(pair, g, parity)
                pool.wait_ge(shifted_done, pair * GROUPS + GROUPS)
                sh.split_q(pool, use, parity, order + 1)
                pool.wait_ge(rden_ready, pair + 1)
                pool.tensor_tensor(av_high[:, :], av_high[:, :], av_low[:, :], ALU.add).then_inc(sh.pool_order, 1)
                pool.wait_ge(sh.pool_order, order + 2)
                pool.wait_ge(sh.o_stored, 16 * (head + 1))
                pool.tensor_tensor(sh.o_head[b][:, cols(i * PAIR, PAIR)], av_high[:, :], rden[:, :],
                                   ALU.mult).then_inc(sh.o_ready, 1)

            over_steps(pool, step)

        @block.vector
        def _(dve):
            def high_part(pair, g, parity):
                dve.wait_ge(expo_ready, pair * GROUPS + g + 3)
                blocks = slice(PER * g, PER * g + PER)
                dve.tensor_copy(high[:, blocks, :], expo[parity][:, blocks, :]).then_inc(high_ready, 1)

            def maximum(tile, u):
                dve.wait_ge(scores_done, tile + 1)
                dve.tensor_reduce(row_max[:, u:u + 1], ps_s[:, 0:N], AX.X, ALU.max).then_inc(max_ready, 1)

            def diagonals(pair, parity):
                dve.wait_ge(max_ready, 2 * pair + 2)
                for u in range(2):
                    last = dve.tensor_scalar(minus_max[parity][:, P * u:P * u + P], cst["ident"][:, :],
                                             row_max[:, u:u + 1], -1.0, ALU.mult, ALU.mult)
                last.then_inc(diagonal_ready, 1)

            for t in (sh.bq_s, sh.bk_s, sh.bv_s):
                dve.memset(t[:, :], 0.0)
            for t in v_stack:
                last = dve.memset(t[:, :, 2 * D:3 * D].bitcast(F32), 1.0)
            last.then_inc(sh.buffers_set, 1)
            for u in range(2):
                maximum(u, u)
            diagonals(0, 0)

            def step(pair, i, parity, h, b, head):
                use = uses(head, i)
                tail = isinstance(i, int)
                dve.wait_ge(sh.bank_filled, use)
                for g in range(3):
                    high_part(pair, g, parity)
                maximum(2 * pair + 2, 0)
                for g in range(3, 6):
                    high_part(pair, g, parity)
                maximum(2 * pair + 3, 1)
                diagonals(pair + 1, 1 - parity)
                for g in range(6, GROUPS):
                    high_part(pair, g, parity)
                dve.wait_ge(sh.bank_kept, (use + 1 if tail else use + 4) + 1)
                dve.reciprocal(rden[:, :], av_sum[:, :]).then_inc(rden_ready, 1)

            over_steps(dve, step)


def output(nc, xs, ao, x1, w_out, b_out, out):
    CW = N // PRE
    CHB = N // CW
    ctx = ExitStack()
    with ctx:
        sb = lambda name, shape, dt=F32: ctx.enter_context(nc.sbuf_tensor("o_" + name, shape, dt))
        sem = lambda name: ctx.enter_context(nc.semaphore("o_" + name))
        w, bias = sb("w", [P, KC, C]), sb("bias", [P, KC])
        a, y = sb("a", [P, KC, B * N]), sb("y", [P, KC, B * N])
        ps = ctx.enter_context(nc.psum_tensor("o_ps", [P, KC, BANK], F32))
        w_loaded, a_loaded = sem("w_loaded"), [sem(f"a_loaded{b}") for b in range(B)]
        proj_done, added, stored = sem("proj_done"), sem("added"), sem("stored")
        block = ctx.enter_context(nc.Block())

        @block.sync
        def _(sync):
            sync.dma_start(w[:, :, :], w_out.rearrange("(k p) o -> p k o", p=P)).then_inc(w_loaded, 16)
            sync.dma_start(bias[:, :], b_out).then_inc(w_loaded, 16)
            for b in range(B):
                for kc in range(KC):
                    for t, src in ((a, ao), (y, x1)):
                        sync.dma_start(t[:, kc, b * N:b * N + N],
                                       src[kc * P:kc * P + P, b * N:b * N + N]).then_inc(a_loaded[b], 16)
            for b in range(B):
                with sync.Fori(0, CHB) as c:
                    sync.wait_ge(added, c + b * CHB + 1)
                    sync.dma_start(out[b].rearrange("(k p) n -> p k n", p=P)[:, :, cols(c * CW, CW)],
                                   y[:, :, cols(c * CW + b * N, CW)]).then_inc(stored, 16)
            sync.wait_ge(stored, 16 * B * CHB)

        @block.tensor
        def _(pe):
            pe.wait_ge(w_loaded, 32)
            for b in range(B):
                pe.wait_ge(a_loaded[b], 64)
                with pe.Fori(0, CHB) as c:
                    pe.wait_ge(added, c + b * CHB)
                    for oc in range(KC):
                        for kc in range(KC):
                            last = pe.matmul(ps[:, oc, 0:CW], w[:, kc, P * oc:P * oc + P],
                                             a[:, kc, cols(c * CW + b * N, CW)], start=kc == 0, stop=kc == KC - 1)
                    last.then_inc(proj_done, 1)

        @block.vector
        def _(dve):
            dve.wait_ge(w_loaded, 32)
            for b in range(B):
                dve.wait_ge(a_loaded[b], 64)
                with dve.Fori(0, CHB) as c:
                    dve.wait_ge(proj_done, c + b * CHB + 1)
                    for oc in range(KC):
                        y_c = y[:, oc, cols(c * CW + b * N, CW)]
                        last = dve.scalar_tensor_tensor(y_c, ps[:, oc, 0:CW], bias[:, oc:oc + 1], y_c,
                                                        ALU.add, ALU.add)
                    last.then_inc(added, 1)


def build(nc, t, out, stop=None):
    ao0 = nc.dram_tensor("ao0", [C, B * N], F32).ap()
    x1 = nc.dram_tensor("x1", [C, B * N], F32).ap()
    ao1 = nc.dram_tensor("ao1", [C, B * N], F32).ap()
    ctx = ExitStack()
    with ctx:
        xs = ctx.enter_context(nc.sbuf_tensor("xs", [P, KC, B, N], F32))
        cst = constants(nc, ctx)
        attention_top(nc, cst, xs, t["x"], t["w_q0"], t["w_k0"], t["w_v0"], t["b_q"], t["b_k"], t["b_v"], ao0)
        mlp(nc, cst, xs, ao0, x1, t["w_o"], t["b_o"], t["w_1"], t["b_1"], t["g_1"], t["be_1"],
            t["w_2"], t["b_2"], t["g_2"], t["be_2"], t["g_rms"])
        attention_full(nc, cst, xs, t["w_q1"], t["w_k1"], t["w_v1"], ao1)
        output(nc, xs, ao1, x1, t["w_out"], t["b_out"], out)


def per_head(w):
    return np.ascontiguousarray(w.reshape(HEADS, D, KC, P).transpose(0, 3, 2, 1))


def per_partition(v, rows=P):
    return np.ascontiguousarray(v.reshape(-1, rows).T)


def kernel(**inputs):
    from concourse import bacc
    from concourse.bass_utils import run_bass_kernel_spmd

    a = {name: np.asarray(v) for name, v in inputs.items()}
    layer0 = {name[len("L0_conv_"):]: v for name, v in a.items() if name.startswith("L0_conv_")}
    qkv = a["L1_conv_w_qkv"]
    arrays = {
        "x": a["x"].reshape(B, C, N),
        "w_q0": per_head(layer0["Wq"]), "w_k0": per_head(layer0["Wk"]), "w_v0": per_head(layer0["Wv"]),
        "b_q": per_partition(layer0["bq"], D), "b_k": per_partition(layer0["bk"], D),
        "b_v": per_partition(layer0["bv"], D),
        "w_o": layer0["Wo"].T, "b_o": per_partition(layer0["bo"]),
        "w_1": layer0["W1"].T, "b_1": per_partition(layer0["b1"]),
        "g_1": per_partition(layer0["g1"]), "be_1": per_partition(layer0["be1"]),
        "w_2": layer0["W2"].T, "b_2": per_partition(layer0["b2"]),
        "g_2": per_partition(layer0["g2"]), "be_2": per_partition(layer0["be2"]),
        "g_rms": per_partition(a["L1_conv_g"]),
        "w_q1": per_head(qkv[0:C]), "w_k1": per_head(qkv[C:2 * C]), "w_v1": per_head(qkv[2 * C:3 * C]),
        "w_out": a["L1_conv_w_out"].T, "b_out": per_partition(a["L1_conv_b_out"]),
    }
    arrays = {name: np.ascontiguousarray(v) for name, v in arrays.items()}
    nc = bacc.Bacc("TRN2", target_bir_lowering=False, num_devices=1)
    t = {name: nc.dram_tensor(name, v.shape, F32, kind="ExternalInput").ap() for name, v in arrays.items()}
    out = nc.dram_tensor("out", [B, C, N], F32, kind="ExternalOutput").ap()
    build(nc, t, out)
    result = run_bass_kernel_spmd(nc, [arrays], core_ids=[0])
    return result.results[0]["out"].reshape(B, C, 48, 48)
```

```python
from contextlib import ExitStack

import numpy as np
import concourse.bass as bass
from concourse import mybir

F32 = mybir.dt.float32
F32R = mybir.dt.float32r
I32 = mybir.dt.int32
ALU = mybir.AluOpType
ACT = mybir.ActivationFunctionType
AX = mybir.AxisListType

P = 128
B, C, N = 2, 256, 48 * 48
KC = C // P
HEADS, D = 8, 32
MLP = 1024
MT = MLP // P
TOPK = 64
BN_EPS = 1e-5
SCALE = float(D) ** -0.5
BANK = 512

PAIR = 2 * P
PAIRS = N // PAIR
MCH = N // P
PRE = 6
PCOLS = N // PRE
PM = PCOLS // P
HEAD_STEPS = B * HEADS
ALL_PAIRS = HEAD_STEPS * PAIRS

CHUNK = 36
CHUNKS = N // CHUNK
KEEP = 3
CAND = CHUNKS * KEEP + 8
ROUNDS = TOPK // 8
LOWEST = -3.0e38
STEEP = 2.0 ** 60

SCOLS = [(c, min(BANK, N - c)) for c in range(0, N, BANK)]
TGROUPS = [(m, min(4, MCH - m)) for m in range(0, MCH, 4)]
NTG = len(TGROUPS)


def cols(start, n):
    return slice(start, start + n) if isinstance(start, int) else bass.ds(start, n)


class Tally:
    semaphore = None


def wait_alone(engine, semaphore, value):
    engine.wait_ge(semaphore, value)
    engine.sem_inc(Tally.semaphore, 1)


def constants(nc, ctx):
    sb = lambda name, shape, dt=F32: ctx.enter_context(nc.sbuf_tensor(name, shape, dt))
    k = {
        "ident": sb("ident", [P, P]),
        "ones": sb("ones", [P, P]),
        "ones_r": sb("ones_r", [P, P], F32R),
        "add_up": sb("add_up", [P, D]),
        "k_low": sb("k_low", [P, 1]),
        "q_low": sb("q_low", [P, 1]),
    }
    made = ctx.enter_context(nc.semaphore("constants_made"))
    Tally.semaphore = ctx.enter_context(nc.semaphore("waits_alone"))
    with nc.Block() as block:

        @block.gpsimd
        def _(pool):
            pool.memset(k["ident"][:, :], 0.0).then_inc(made, 1)
            pool.wait_ge(made, 1)
            pool.affine_select(out=k["ident"][:, :], in_=k["ident"][:, :], compare_op=ALU.not_equal,
                               fill=1.0, base=0, pattern=[[-1, P]],
                               channel_multiplier=1).then_inc(made, 1)

        @block.vector
        def _(dve):
            dve.memset(k["ones"][:, :], 1.0)
            dve.memset(k["ones_r"][:, :].bitcast(F32), 1.0)
            for quadrant in range(4):
                rows = slice(D * quadrant, D * quadrant + D)
                dve.memset(k["k_low"][rows, :], float(quadrant >= 2))
                dve.memset(k["q_low"][rows, :], float(quadrant % 2))
            dve.wait_ge(made, 2)
            for quadrant in range(4):
                rows = slice(D * quadrant, D * quadrant + D)
                dve.tensor_copy(k["add_up"][rows, :], k["ident"][rows, rows])
    return k


def over_steps(engine, step):
    with engine.Fori(0, HEADS) as h:
        for b in range(B):
            head = h * B + b
            with engine.Fori(0, PRE // 2) as half:
                for r in range(2):
                    step(head * PAIRS + half * 2 + r, half * 2 + r, (b + r) % 2, h, b, head)
            for i in range(PRE, PAIRS):
                step(head * PAIRS + i, i, (b + i) % 2, h, b, head)


class BankUses:

    def __init__(self, plain, preparing, before):
        self.plain, self.preparing, self.before = plain, preparing, before
        self.head = PRE * preparing + (PAIRS - PRE) * plain

    def __call__(self, head, i):
        if isinstance(i, int) and i >= PRE:
            return head * self.head + self.before + PRE * self.preparing + (i - PRE) * self.plain
        return head * self.head + self.before + i * self.preparing


def load_projections(sync, w_s, drams, h, loaded):
    for t, w in zip(w_s, drams):
        for r in range(t.shape[2] // D):
            sync.dma_start(t[:, :, D * r:D * r + D], w[h]).then_inc(loaded, 16)


class Shared:

    def __init__(self, nc, ctx, cst, xs, name, ahead, uses, q_use):
        sb = lambda n, shape, dt=F32: ctx.enter_context(nc.sbuf_tensor(name + n, shape, dt))
        sem = lambda n: ctx.enter_context(nc.semaphore(name + n))
        self.cst, self.xs, self.uses, self.q_use = cst, xs, uses, q_use
        self.ahead = ahead
        self.wq_s, self.wk_s, self.wv_s = sb("wq", [P, KC, 4 * D]), sb("wk", [P, KC, 4 * D]), sb("wv", [P, KC, D])
        self.bq_s, self.bk_s, self.bv_s = sb("bq", [P, HEADS + 1]), sb("bk", [P, HEADS + 1]), sb("bv", [D, HEADS + 1])
        self.k_raw, self.k_part = sb("k_raw", [P, PCOLS]), sb("k_part", [P, PCOLS], F32R)
        self.q_raw, self.q_part = sb("q_raw", [P, PAIR]), sb("q_part", [P, PAIR], F32R)
        self.k_stack = [sb(f"k_stack{n}", [P, N], F32R) for n in range(2)]
        self.q_stack = [sb(f"q_stack{n}", [P, PAIR], F32R) for n in range(2)]
        self.v_cols = sb("v_cols", [D, PCOLS])
        self.o_head = [sb(f"o_head{n}", [D, N]) for n in range(2)]
        self.bank = ctx.enter_context(nc.psum_tensor(name + "bank", [P, BANK], F32))
        self.x_loaded, self.bias_loaded = sem("x_loaded"), sem("bias_loaded")
        self.wq_loaded, self.wkv_loaded = sem("wq_loaded"), sem("wkv_loaded")
        self.buffers_set = sem("buffers_set")
        self.bank_filled, self.bank_kept = sem("bank_filled"), sem("bank_kept")
        self.k_stack_ready, self.q_stack_ready = sem("k_stack_ready"), sem("q_stack_ready")
        self.o_ready, self.o_stored = sem("o_ready"), sem("o_stored")
        self.pool_order = sem("pool_order")

    def load_first(self, sync, w_q, w_k, w_v, biases):
        load_projections(sync, (self.wk_s, self.wv_s), (w_k, w_v), 0, self.wkv_loaded)
        load_projections(sync, (self.wq_s,), (w_q,), 0, self.wq_loaded)
        if biases:
            sync.wait_ge(self.buffers_set, 1)
            for t, src in zip((self.bq_s, self.bk_s, self.bv_s), biases):
                for r in range(t.shape[0] // D):
                    sync.dma_start(t[D * r:D * r + D, 0:HEADS],
                                   src).then_inc(self.bias_loaded, 16)

    def load_and_store(self, sync, w_q, w_k, w_v, ao, wait_written):
        sync.sem_inc(self.o_stored, 32)

        def store(h, b):
            wait_written(h * B + b)
            wait_alone(sync, self.o_stored, 32 + (h * B + b) * 16)
            sync.dma_start(ao.rearrange("(h d) n -> h d n", d=D)[h, :, b * N:b * N + N],
                           self.o_head[b][:, :]).then_inc(self.o_stored, 16)

        def per_head(h, h_next):
            sync.wait_ge(self.bank_filled, self.uses(h * B, PRE))
            load_projections(sync, (self.wk_s, self.wv_s), (w_k, w_v), h_next, self.wkv_loaded)
            store(h, 0)
            sync.wait_ge(self.bank_filled, self.uses(h * B + 1, PAIRS - self.ahead - 1) + self.q_use + 1)
            load_projections(sync, (self.wq_s,), (w_q,), h_next, self.wq_loaded)
            store(h, 1)

        with sync.Fori(0, HEADS - 1) as h:
            per_head(h, h + 1)
        per_head(HEADS - 1, HEADS - 1)
        sync.wait_ge(self.o_stored, 32 + 16 * HEAD_STEPS)

    def bank_free(self, pe, use):
        if not (isinstance(use, int) and use == 0):
            wait_alone(pe, self.bank_kept, use)

    def project(self, pe, use, out, weights, b, col, n):
        self.bank_free(pe, use)
        for kc in range(KC):
            last = pe.matmul(out, weights[:, kc, :], self.xs[:, kc, b, cols(col, n)],
                             start=kc == 0, stop=kc == KC - 1)
        last.then_inc(self.bank_filled, 1)

    def project_q(self, pe, use, b, i):
        self.project(pe, use, self.bank[:, 0:PAIR], self.wq_s, b, i * PAIR, PAIR)

    def project_k(self, pe, use, b, c):
        self.project(pe, use, self.bank[:, 0:PCOLS], self.wk_s, b, c * PCOLS, PCOLS)

    def project_v(self, pe, use, b, c):
        self.project(pe, use, self.bank[0:D, 0:PCOLS], self.wv_s, b, c * PCOLS, PCOLS)

    def turn_v(self, pe, use):
        self.bank_free(pe, use)
        for m in range(PM):
            last = pe.transpose(self.bank[:, D * m:D * m + D], self.v_cols[:, P * m:P * m + P],
                                self.cst["ident"][0:D, 0:D])
        last.then_inc(self.bank_filled, 1)

    def keep(self, act, use, out, rows, n, bias):
        wait_alone(act, self.bank_filled, use + 1)
        act.activation(out, self.bank[0:rows, 0:n], ACT.Identity, bias=bias).then_inc(self.bank_kept, 1)

    def keep_q(self, act, use, h, pairs_before):
        if not (isinstance(pairs_before, int) and pairs_before == 0):
            act.wait_ge(self.q_stack_ready, pairs_before)
        self.keep(act, use, self.q_raw[:, :], P, PAIR, self.bq_s[:, cols(h, 1)])

    def keep_k(self, act, use, h, chunks_before):
        if not (isinstance(chunks_before, int) and chunks_before == 0):
            act.wait_ge(self.k_stack_ready, chunks_before)
        self.keep(act, use, self.k_raw[:, :], P, PCOLS, self.bk_s[:, cols(h, 1)])

    def keep_v(self, act, use, h):
        self.keep(act, use, self.v_cols[:, :], D, PCOLS, self.bv_s[:, cols(h, 1)])

    def split(self, pool, raw, low, part, out, order, done):
        pool.tensor_scalar(part, raw, 0.0, low[:, 0:1], ALU.add, ALU.mult).then_inc(self.pool_order, 1)
        pool.wait_ge(self.pool_order, order)
        pool.tensor_tensor(out, raw, part.bitcast(F32), ALU.subtract).then_inc(done, 1)

    def split_k(self, pool, use, b, c, order):
        wait_alone(pool, self.bank_kept, use + 1)
        self.split(pool, self.k_raw[:, :], self.cst["k_low"], self.k_part[:, :],
                   self.k_stack[b][:, cols(c * PCOLS, PCOLS)], order, self.k_stack_ready)

    def split_q(self, pool, use, parity, order):
        wait_alone(pool, self.bank_kept, use + 1)
        self.split(pool, self.q_raw[:, :], self.cst["q_low"], self.q_part[:, :],
                   self.q_stack[parity][:, :], order, self.q_stack_ready)


def attention_top(nc, cst, xs, x, w_q, w_k, w_v, b_q, b_k, b_v, ao):
    ctx = ExitStack()
    with ctx:
        sb = lambda name, shape, dt=F32: ctx.enter_context(nc.sbuf_tensor("a_" + name, shape, dt))
        sem = lambda name: ctx.enter_context(nc.semaphore("a_" + name))
        uses = BankUses(plain=3, preparing=4, before=PRE + 3)
        sh = Shared(nc, ctx, cst, xs, "a_", 3, uses, 0)
        v_s = [sb(f"v{n}", [P, MCH, D]) for n in range(2)]
        scores = [sb(f"scores{n}", [P, N]) for n in range(4)]
        probs = [sb(f"probs{n}", [P, N]) for n in range(2)]
        probs_t = [sb(f"probs_t{n}", [P, MCH, P]) for n in range(2)]
        scratch = sb("scratch", [P, N])
        top8 = sb("top8", [P, 2, CHUNKS + 1, 8])
        cand = sb("cand", [P, 2, CAND])
        best = sb("best", [P, 2, TOPK])
        missed = sb("missed", [P, 2])
        flag, flag_t, flags = sb("flag", [P, D]), sb("flag_t", [P, D]), sb("flags", [1, P])
        any_missed = sb("any_missed", [1, 1], I32)
        steep_kth = [sb(f"steep_kth{n}", [P, 2]) for n in range(2)]
        minus_max = [sb(f"minus_max{n}", [P, 2]) for n in range(2)]
        above = sb("above", [P, 2])
        sums, one_by_sum = sb("sums", [P, 2]), sb("one_by_sum", [P, 2])
        diagonal = [sb(f"diagonal{n}", [P, P]) for n in range(2)]
        parts = sb("parts", [P, PAIR])

        ps_s = ctx.enter_context(nc.psum_tensor("a_ps_s", [P, 5 * BANK], F32))
        ps_t = [ctx.enter_context(nc.psum_tensor(f"a_ps_t{n}", [P, BANK], F32)) for n in range(2)]

        scores_done, scores_kept = sem("scores_done"), sem("scores_kept")
        kth_ready = sem("kth_ready")
        penalty_ready, masked_ready, probs_ready = sem("penalty_ready"), sem("masked_ready"), sem("probs_ready")
        turned, turned_kept = sem("turned"), sem("turned_kept")
        diagonal_ready = sem("diagonal_ready")
        v_projected, v_cols_kept, v_turned, v_kept = (sem("v_projected"), sem("v_cols_kept"), sem("v_turned"),
                                                      sem("v_kept"))
        tops_taken, dve_order = sem("tops_taken"), sem("dve_order")

        block = ctx.enter_context(nc.Block())

        @block.sync
        def _(sync):
            for b in range(B):
                for kc in range(KC):
                    sync.dma_start(xs[:, kc, b, :], x[b, kc * P:kc * P + P, :]).then_inc(sh.x_loaded, 16)
            sh.load_first(sync, w_q, w_k, w_v, (b_q, b_k, b_v))
            sh.load_and_store(sync, w_q, w_k, w_v, ao,
                              lambda head: sync.wait_ge(sh.bank_kept, uses(head, PAIRS)))

        @block.tensor
        def _(pe):
            def score(tile, u, parity, b, first=False):
                if not first:
                    pe.wait_ge(scores_kept, tile)
                for c, n in SCOLS:
                    last = pe.matmul(ps_s[:, c:c + n], sh.q_stack[parity][:, P * u:P * u + P],
                                     sh.k_stack[b][:, c:c + n], start=True, stop=True)
                last.then_inc(scores_done, 1)

            def turn(u, g):
                m0, n = TGROUPS[g]
                bank = ps_t[(NTG * u + g) % 2]
                for m in range(n):
                    last = pe.matmul(bank[:, P * m:P * m + P], probs[u][:, P * (m0 + m):P * (m0 + m) + P],
                                     diagonal[u][:, :], start=True, stop=True)
                last.then_inc(turned, 1)

            def weigh(tile, u, g, b):
                pe.wait_ge(turned_kept, tile * NTG + g + 1)
                m0, n = TGROUPS[g]
                for m in range(m0, m0 + n):
                    rows = slice(D * (m % 4), D * (m % 4) + D)
                    last = pe.matmul(sh.bank[rows, P * u:P * u + P], v_s[b][:, m, :], probs_t[u][:, m, :],
                                     start=m < 4, stop=m + 4 >= MCH)
                return last

            pe.wait_ge(sh.x_loaded, 16 * B * KC)
            def project_v(b, c):
                for kc in range(KC):
                    last = pe.matmul(ps_t[0][0:D, 0:PCOLS], sh.wv_s[:, kc, :], xs[:, kc, b, cols(c * PCOLS, PCOLS)],
                                     start=kc == 0, stop=kc == KC - 1)
                last.then_inc(v_projected, 1)

            def turn_v(n):
                wait_alone(pe, v_cols_kept, n + 1)
                for m in range(PM):
                    last = pe.transpose(ps_t[1][:, D * m:D * m + D], sh.v_cols[:, P * m:P * m + P],
                                        cst["ident"][0:D, 0:D])
                last.then_inc(v_turned, 1)

            pe.wait_ge(sh.wkv_loaded, 80)
            for c in range(PRE):
                project_v(0, c)
                sh.project_k(pe, c, 0, c)
                turn_v(c)
                pe.wait_ge(v_kept, c + 1)
            pe.wait_ge(sh.wq_loaded, 64)
            for n in range(3):
                sh.project_q(pe, PRE + n, 0, n)
            pe.wait_ge(sh.k_stack_ready, PRE)
            for n in range(2):
                pe.wait_ge(sh.q_stack_ready, n + 1)
                for u in range(2):
                    score(2 * n + u, u, n, 0, first=n + u == 0)
            pe.wait_ge(sh.q_stack_ready, 3)
            score(4, 0, 0, 0)

            def step(pair, i, parity, h, b, head):
                use = uses(head, i)
                tail = isinstance(i, int)
                if tail and i + 3 == PAIRS:
                    pe.wait_ge(sh.wq_loaded, 64 * (h + b + 1))
                if tail and i + 3 >= PAIRS:
                    sh.project_q(pe, use, 1 - b, i + 3 - PAIRS)
                else:
                    sh.project_q(pe, use, b, i + 3)
                if not tail:
                    chunk = (head + 1) * PRE + i
                    wait_alone(pe, sh.wkv_loaded, 80 * (h + b + 1))
                    project_v(1 - b, i)
                    sh.project_k(pe, use + 1, 1 - b, i)
                    turn_v(chunk)
                use = use + (1 if tail else 2)
                pe.wait_ge(diagonal_ready, 2 * pair + 1)
                turn(0, 0)
                if not tail:
                    pe.wait_ge(v_kept, chunk + 1)
                turn(0, 1)
                score(2 * pair + 5, 1, parity, 1 - b if tail and i + 2 >= PAIRS else b)
                sh.bank_free(pe, use)
                for g in range(NTG):
                    weigh(2 * pair, 0, g, b)
                    if g + 2 < NTG:
                        turn(0, g + 2)
                    if g == 3:
                        if tail and i + 3 == PAIRS:
                            pe.wait_ge(sh.k_stack_ready, (head + 2) * PRE)
                        pe.wait_ge(sh.q_stack_ready, pair + 4)
                        score(2 * pair + 6, 0, 1 - parity, 1 - b if tail and i + 3 >= PAIRS else b)
                        pe.wait_ge(diagonal_ready, 2 * pair + 2)
                        turn(1, 0)
                turn(1, 1)
                for g in range(NTG):
                    last = weigh(2 * pair + 1, 1, g, b)
                    if g + 2 < NTG:
                        turn(1, g + 2)
                last.then_inc(sh.bank_filled, 1)
                sh.bank_free(pe, use + 1)
                pe.matmul(sh.bank[0:D, 0:PAIR], cst["add_up"][:, :], parts[:, :], start=True,
                          stop=True).then_inc(sh.bank_filled, 1)

            over_steps(pe, step)

        @block.scalar
        def _(act):
            def keep_v_cols(h, n):
                wait_alone(act, v_projected, n + 1)
                act.activation(sh.v_cols[:, :], ps_t[0][0:D, 0:PCOLS], ACT.Identity,
                               bias=sh.bv_s[:, cols(h, 1)]).then_inc(v_cols_kept, 1)

            def keep_v(b, c, n):
                wait_alone(act, v_turned, n + 1)
                act.activation(v_s[b][:, cols(c * PM, PM), :],
                               ps_t[1][:, 0:PM * D].rearrange("p (m d) -> p m d", d=D),
                               ACT.Copy).then_inc(v_kept, 1)

            def keep_scores(tile, n):
                act.wait_ge(scores_done, tile + 1)
                act.activation(scores[n][:, :], ps_s[:, 0:N], ACT.Copy).then_inc(scores_kept, 1)

            act.wait_ge(sh.bias_loaded, 16 * 9)
            for c in range(PRE):
                keep_v_cols(0, c)
                sh.keep_k(act, c, 0, c)
                keep_v(0, c, c)
            for n in range(3):
                sh.keep_q(act, PRE + n, 0, n)
            for n in range(4):
                keep_scores(n, n)

            def exponentials(tile, u, parity):
                act.wait_ge(masked_ready, tile + 1)
                act.activation(probs[u][:, :], probs[u][:, :], ACT.Exp, scale=SCALE,
                               bias=minus_max[parity][:, u:u + 1], accum_out=sums[:, u:u + 1]
                               ).then_inc(probs_ready, 1)

            def keep_turned(tile, u, g):
                m0, n = TGROUPS[g]
                act.wait_ge(turned, tile * NTG + g + 1)
                act.activation(probs_t[u][:, m0:m0 + n, :],
                               ps_t[(NTG * u + g) % 2][:, 0:n * P].rearrange("p (m q) -> p m q", q=P),
                               ACT.Copy).then_inc(turned_kept, 1)

            def penalty(u, parity):
                act.activation(probs[u][:, :], scores[2 * parity + u][:, :], ACT.Relu, scale=-STEEP,
                               bias=steep_kth[parity][:, u:u + 1]).then_inc(penalty_ready, 1)

            act.wait_ge(kth_ready, 1)
            for u in range(2):
                penalty(u, 0)

            def step(pair, i, parity, h, b, head):
                use = uses(head, i)
                tail = isinstance(i, int)
                chunk = (head + 1) * PRE + i
                exponentials(2 * pair, 0, parity)
                sh.keep_q(act, use, h + b if tail and i + 3 >= PAIRS else h, pair + 3)
                if not tail:
                    keep_v_cols(h + b, chunk)
                keep_scores(2 * pair + 4, 2 * parity)
                if not tail:
                    sh.keep_k(act, use + 1, h + b, chunk)
                    keep_v(1 - b, i, chunk)
                use = use + (1 if tail else 2)
                for g in range(2):
                    keep_turned(2 * pair, 0, g)
                exponentials(2 * pair + 1, 1, parity)
                keep_turned(2 * pair, 0, 2)
                keep_scores(2 * pair + 5, 2 * parity + 1)
                for g in range(3, NTG):
                    keep_turned(2 * pair, 0, g)
                keep_turned(2 * pair + 1, 1, 0)
                act.wait_ge(kth_ready, pair + 2)
                penalty(0, 1 - parity)
                for g in range(1, NTG):
                    keep_turned(2 * pair + 1, 1, g)
                act.wait_ge(sh.bank_filled, use + 1)
                act.activation(parts[:, :], sh.bank[:, 0:PAIR], ACT.Copy).then_inc(sh.bank_kept, 1)
                penalty(1, 1 - parity)
                wait_alone(act, sh.o_stored, 16 * (head + 1))
                wait_alone(act, sh.bank_filled, use + 2)
                act.activation(sh.o_head[b][:, cols(i * PAIR, PAIR)], sh.bank[0:D, 0:PAIR],
                               ACT.Copy).then_inc(sh.bank_kept, 1)

            over_steps(act, step)

        @block.gpsimd
        def _(pool):
            for c in range(PRE):
                sh.split_k(pool, c, 0, c, c + 1)
            for n in range(3):
                if n == 2:
                    pool.wait_ge(scores_done, 2)
                sh.split_q(pool, PRE + n, n % 2, PRE + n + 1)

            def step(pair, i, parity, h, b, head):
                use = uses(head, i)
                tail = isinstance(i, int)
                splits = PRE + 3 + head * (PAIRS + PRE) + (PRE + i if tail else i * 2)
                for u in range(2):
                    pool.wait_ge(penalty_ready, 2 * pair + u + 1)
                    pool.tensor_tensor(probs[u][:, :], scores[2 * parity + u][:, :], probs[u][:, :],
                                       ALU.subtract).then_inc(masked_ready, 1)
                pool.wait_ge(scores_done, 2 * pair + 4)
                sh.split_q(pool, use, 1 - parity, splits + 1)
                if not tail:
                    sh.split_k(pool, use + 1, 1 - b, i, splits + 2)

            over_steps(pool, step)

        @block.vector
        def _(dve):
            at = {"n": 0}

            def counted(instruction):
                at["n"] += 1
                instruction.then_inc(dve_order, 1)
                return at["n"]

            def chunk_tops(pair, parity, u, between=lambda c: None):
                wait_alone(dve, scores_kept, 2 * pair + u + 1)
                for c in range(CHUNKS):
                    last = dve.max(top8[:, u, c, :], scores[2 * parity + u][:, CHUNK * c:CHUNK * c + CHUNK])
                    if c < CHUNKS - 1:
                        between(c)
                last.then_inc(tops_taken, 1)

            def one_by_sums(pair, u):
                wait_alone(dve, probs_ready, 2 * pair + u + 1)
                return counted(dve.reciprocal(one_by_sum[:, u:u + 1], sums[:, u:u + 1]))

            def diagonals(u):
                dve.tensor_scalar(diagonal[u][:, :], cst["ident"][:, :], one_by_sum[:, u:u + 1], None,
                                  ALU.mult).then_inc(diagonal_ready, 1)

            def select(pair):
                at["n"] = 0
                after = lambda n: dve.wait_ge(dve_order, n)
                wait_alone(dve, tops_taken, 2 * pair + 2)
                rest, written = [0, 0], [0, 0]
                for u in range(2):
                    rest[u] = counted(dve.max(top8[:, u, CHUNKS, :], top8[:, u, 0:CHUNKS, KEEP:8]))
                    counted(dve.tensor_copy(cand[:, u, 0:CHUNKS * KEEP].rearrange("p (c k) -> p c k", k=KEEP),
                                            top8[:, u, 0:CHUNKS, 0:KEEP]))
                for u in range(2):
                    after(rest[u])
                    written[u] = counted(dve.tensor_copy(cand[:, u, CHUNKS * KEEP:CAND], top8[:, u, CHUNKS, :]))
                counted(dve.tensor_reduce(missed[:, :], top8[:, :, :, 7], AX.X, ALU.max))
                for r in range(ROUNDS):
                    found = [0, 0]
                    for u in range(2):
                        after(written[u])
                        found[u] = counted(dve.max(best[:, u, 8 * r:8 * r + 8], cand[:, u, :]))
                    previous = not (isinstance(pair, int) and pair == 0)
                    if previous and r == 3:
                        summed = one_by_sums(pair - 1, 0)
                    if r < ROUNDS - 1:
                        for u in range(2):
                            after(found[u])
                            written[u] = counted(dve.match_replace(cand[:, u, :], best[:, u, 8 * r:8 * r + 8],
                                                                   cand[:, u, :], LOWEST))
                    if previous and r == 3:
                        after(summed)
                        diagonals(0)

            def any_of(marks, stage):
                if stage == 0:
                    return dve.tensor_reduce(flag[:, 0:1], marks, AX.X, ALU.max)
                if stage == 1:
                    return dve.transpose(flag_t[:, :], flag[:, :])
                if stage == 2:
                    for q in range(4):
                        last = dve.tensor_copy(flags[:, D * q:D * q + D], flag_t[D * q:D * q + 1, :])
                    return last
                return dve.tensor_reduce(any_missed[:, :], flags[:, :], AX.X, ALU.max)

            def check(c):
                if c in (1, 3, 5, 7, 9):
                    dve.wait_ge(dve_order, at["n"])
                    if c == 1:
                        counted(dve.tensor_tensor(missed[:, :], missed[:, :], best[:, :, TOPK - 1], ALU.is_gt))
                    else:
                        counted(any_of(missed[:, :], (c - 3) // 2))

            def hand_on(pair, parity):
                dve.wait_ge(dve_order, at["n"])
                doubtful = dve.value_load(any_missed[0:1, 0:1], min_val=0, max_val=1)
                dve.sem_clear(dve_order)
                with dve.If(doubtful > 0):
                    for u in range(2):
                        dve.tensor_scalar(scratch[:, :], scores[2 * parity + u][:, :],
                                          best[:, u, TOPK - 1:TOPK], None, ALU.is_gt, ALU.add,
                                          accum_out=above[:, u:u + 1])
                        dve.drain()
                    dve.tensor_scalar(above[:, :], above[:, :], TOPK - 0.5, None, ALU.is_gt)
                    for stage in range(4):
                        dve.drain()
                        any_of(above[:, :], stage)
                    dve.drain()
                    again = dve.value_load(any_missed[0:1, 0:1], min_val=0, max_val=1)
                    with dve.If(again > 0):
                        for u in range(2):
                            for stage in range(4):
                                dve.drain()
                                any_of(above[:, u:u + 1], stage)
                            dve.drain()
                            tile_again = dve.value_load(any_missed[0:1, 0:1], min_val=0, max_val=1)
                            with dve.If(tile_again > 0):
                                dve.tensor_copy(scratch[:, :], scores[2 * parity + u][:, :])
                                for r in range(ROUNDS):
                                    dve.drain()
                                    dve.max(best[:, u, 8 * r:8 * r + 8], scratch[:, :])
                                    dve.drain()
                                    if r < ROUNDS - 1:
                                        dve.match_replace(scratch[:, :], best[:, u, 8 * r:8 * r + 8],
                                                          scratch[:, :], LOWEST)
                dve.tensor_scalar(steep_kth[parity][:, :], best[:, :, TOPK - 1], STEEP, None, ALU.mult)
                dve.tensor_scalar(minus_max[parity][:, :], best[:, :, 0], -SCALE, None,
                                  ALU.mult).then_inc(kth_ready, 1)

            def pair_step(pair, parity):
                chunk_tops(pair, parity, 1)
                select(pair)

                def between(c):
                    check(c)
                    if not (isinstance(pair, int) and pair == 0):
                        if c == 24:
                            one_by_sums(pair - 1, 1)
                        if c == 26:
                            dve.wait_ge(dve_order, at["n"])
                            diagonals(1)

                chunk_tops(pair + 1, 1 - parity, 0, between)
                hand_on(pair, parity)

            for t in (sh.bq_s, sh.bk_s, sh.bv_s, flag):
                last = dve.memset(t[:, :], 0.0)
            last.then_inc(sh.buffers_set, 1)
            dve.wait_ge(sh.buffers_set, 1)
            chunk_tops(0, 0, 0)
            pair_step(0, 0)
            with dve.Fori(0, (ALL_PAIRS - 2) // 2) as k:
                pair_step(k * 2 + 1, 1)
                pair_step(k * 2 + 2, 0)
            pair_step(ALL_PAIRS - 1, 1)
            at["n"] = 0
            for u in range(2):
                dve.wait_ge(dve_order, one_by_sums(ALL_PAIRS - 1, u))
                diagonals(u)
            dve.sem_inc(kth_ready, 1)


def mlp(nc, cst, xs, ao, x1, w_o, b_o, w_1, b_1, g_1, be_1, w_2, b_2, g_2, be_2, g_rms):
    CW = BANK
    NCH = B * N // CW
    ctx = ExitStack()
    with ctx:
        sb = lambda name, shape, dt=F32: ctx.enter_context(nc.sbuf_tensor("m_" + name, shape, dt))
        sem = lambda name: ctx.enter_context(nc.semaphore("m_" + name))
        hid = sb("hid", [P, NCH, MT, CW])
        w = sb("w", [P, KC * MLP])
        w1_s = w[:, :].rearrange("p (k m) -> p k m", k=KC)
        w2_s = w[:, :].rearrange("p (k c) -> p k c", k=MT)
        wo_s = sb("wo", [P, KC, C])
        vec = {n: sb(n, [P, m]) for n, m in (("b_o", KC), ("b_1", MT), ("g_1", MT), ("be_1", MT), ("b_2", KC),
                                             ("g_2", KC), ("be_2", KC), ("g_rms", KC))}
        stats1, mean1 = sb("stats1", [P, MT, NCH * 6]), sb("mean1", [P, MT, 2])
        stats2, mean2 = sb("stats2", [P, KC, NCH * 6]), sb("mean2", [P, KC, 2])
        scale1, shift1 = sb("scale1", [P, MT]), sb("shift1", [P, MT])
        scale2, shift2 = sb("scale2", [P, KC]), sb("shift2", [P, KC])
        ps_o = ctx.enter_context(nc.psum_tensor("m_ps_o", [P, KC, BANK], F32))
        ps_h = [ctx.enter_context(nc.psum_tensor(f"m_ps_h{n}", [P, BANK], F32)) for n in range(4)]
        xf = xs[:, :, :, :].rearrange("p k b n -> p k (b n)")

        first_ao_loaded, ao_loaded = sem("first_ao_loaded"), sem("ao_loaded")
        w1_loaded, w2_loaded, vec_loaded = sem("w1_loaded"), sem("w2_loaded"), sem("vec_loaded")
        proj_done, o_ready = sem("proj_done"), sem("o_ready")
        hid_done, hid_kept = sem("hid_done"), sem("hid_kept")
        var1_ready, dev1_ready, bn1_ready, bn_order = (sem("var1_ready"), sem("dev1_ready"), sem("bn1_ready"),
                                                       sem("bn_order"))
        relu_done, y_done, y_kept = sem("relu_done"), sem("y_done"), sem("y_kept")
        var2_ready, dev2_ready, bn2_ready = sem("var2_ready"), sem("dev2_ready"), sem("bn2_ready")
        y_scaled, x1_ready, x1_stored = sem("y_scaled"), sem("x1_ready"), sem("x1_stored")
        squares_ready, sums_done, norm_ready = sem("squares_ready"), sem("sums_done"), sem("norm_ready")
        xn_order, xn_ready = sem("xn_order"), sem("xn_ready")
        block = ctx.enter_context(nc.Block())

        def ao_slot(c, n):
            return hid[:, cols(c, n), MT - KC:MT, :]

        @block.sync
        def _(sync):
            sync.dma_start(wo_s[:, :, :], w_o.rearrange("(k p) o -> p k o", p=P)).then_inc(first_ao_loaded, 16)
            for kc in range(KC):
                src = ao[kc * P:kc * P + P, :].rearrange("p (c n) -> p c n", n=CW)
                sync.dma_start(hid[:, 0, MT - KC + kc, :], src[:, 0, :]).then_inc(first_ao_loaded, 16)
            for kc in range(KC):
                src = ao[kc * P:kc * P + P, :].rearrange("p (c n) -> p c n", n=CW)
                sync.dma_start(hid[:, 1:NCH, MT - KC + kc, :], src[:, 1:NCH, :]).then_inc(ao_loaded, 16)
            sync.dma_start(w1_s, w_1.rearrange("(k p) o -> p k o", p=P)).then_inc(w1_loaded, 16)
            for name, src in (("b_o", b_o), ("b_1", b_1), ("g_1", g_1), ("be_1", be_1), ("b_2", b_2),
                              ("g_2", g_2), ("be_2", be_2), ("g_rms", g_rms)):
                sync.dma_start(vec[name][:, :], src).then_inc(vec_loaded, 16)
            sync.wait_ge(hid_done, NCH * MT)
            sync.dma_start(w2_s, w_2.rearrange("(k p) o -> p k o", p=P)).then_inc(w2_loaded, 16)
            sync.wait_ge(x1_ready, NCH)
            for kc in range(KC):
                sync.dma_start(x1[kc * P:kc * P + P, :].rearrange("p (c n) -> p c n", n=CW),
                               hid[:, :, kc, :]).then_inc(x1_stored, 16)
            sync.wait_ge(x1_stored, 16 * KC)

        @block.tensor
        def _(pe):
            def project(c):
                pe.wait_ge(o_ready, c)
                for oc in range(KC):
                    for kc in range(KC):
                        last = pe.matmul(ps_o[:, oc, :], wo_s[:, kc, P * oc:P * oc + P],
                                         hid[:, c, MT - KC + kc, :], start=kc == 0, stop=kc == KC - 1)
                last.then_inc(proj_done, 1)

            def hidden(c):
                pe.wait_ge(o_ready, c + 1)
                for mt in range(MT):
                    pe.wait_ge(hid_kept, c * MT + mt + 1)
                    for kc in range(KC):
                        last = pe.matmul(ps_h[mt % 4][:, :], w1_s[:, kc, P * mt:P * mt + P],
                                         xf[:, kc, cols(c * CW, CW)], start=kc == 0, stop=kc == KC - 1)
                    last.then_inc(hid_done, 1)

            pe.wait_ge(first_ao_loaded, 16 * 3)
            for oc in range(KC):
                for kc in range(KC):
                    last = pe.matmul(ps_o[:, oc, :], wo_s[:, kc, P * oc:P * oc + P], hid[:, 0, MT - KC + kc, :],
                                     start=kc == 0, stop=kc == KC - 1)
            last.then_inc(proj_done, 1)
            pe.wait_ge(ao_loaded, 16 * KC)
            pe.wait_ge(w1_loaded, 16)
            with pe.Fori(0, NCH - 1) as c:
                project(c + 1)
                hidden(c)
            hidden(NCH - 1)

            pe.wait_ge(w2_loaded, 16)
            with pe.Fori(0, NCH) as c:
                for oc in range(KC):
                    pe.wait_ge(y_kept, c * KC + oc + 1)
                    for mt in range(MT):
                        if oc == 0:
                            pe.wait_ge(relu_done, c * MT + mt + 1)
                        last = pe.matmul(ps_o[:, oc, :], w2_s[:, mt, P * oc:P * oc + P], hid[:, c, mt, :],
                                         start=mt == 0, stop=mt == MT - 1)
                    last.then_inc(y_done, 1)

            with pe.Fori(0, NCH) as c:
                pe.wait_ge(squares_ready, c + 1)
                pe.wait_ge(norm_ready, c + 1)
                for kc in range(KC):
                    last = pe.matmul(ps_h[0][:, :], cst["ones"][:, :], hid[:, c, KC + kc, :],
                                     start=kc == 0, stop=kc == KC - 1)
                last.then_inc(sums_done, 1)

        @block.scalar
        def _(act):
            act.sem_inc(hid_kept, 4)
            act.sem_inc(y_kept, KC)
            act.sem_inc(norm_ready, 1)
            act.wait_ge(vec_loaded, 16 * 8)
            with act.Fori(0, NCH) as c:
                for mt in range(MT):
                    act.wait_ge(hid_done, c * MT + mt + 1)
                    act.activation(hid[:, c, mt, :], ps_h[mt % 4][:, :], ACT.Identity,
                                   bias=vec["b_1"][:, mt:mt + 1]).then_inc(hid_kept, 1)
            act.wait_ge(var1_ready, 1)
            act.activation(mean1[:, :, 1], mean1[:, :, 1], ACT.Sqrt).then_inc(dev1_ready, 1)
            act.wait_ge(bn1_ready, 1)

            def relu(c):
                for mt in range(MT):
                    act.activation(hid[:, c, mt, :], hid[:, c, mt, :], ACT.Relu, scale=scale1[:, mt:mt + 1],
                                   bias=shift1[:, mt:mt + 1]).then_inc(relu_done, 1)

            def keep_y(c):
                for oc in range(KC):
                    act.wait_ge(y_done, c * KC + KC)
                    act.activation(hid[:, c, oc, :], ps_o[:, oc, :], ACT.Identity,
                                   bias=vec["b_2"][:, oc:oc + 1]).then_inc(y_kept, 1)

            relu(0)
            with act.Fori(0, NCH - 1) as c:
                relu(c + 1)
                keep_y(c)
            keep_y(NCH - 1)
            act.wait_ge(var2_ready, 1)
            act.activation(mean2[:, :, 1], mean2[:, :, 1], ACT.Sqrt).then_inc(dev2_ready, 1)
            act.wait_ge(bn2_ready, 1)
            with act.Fori(0, NCH) as c:
                for kc in range(KC):
                    last = act.activation(hid[:, c, kc, :], hid[:, c, kc, :], ACT.Identity,
                                          scale=scale2[:, kc:kc + 1], bias=shift2[:, kc:kc + 1])
                last.then_inc(y_scaled, 1)
            with act.Fori(0, NCH) as c:
                act.wait_ge(x1_ready, c + 1)
                act.activation(hid[:, c, KC:2 * KC, :], hid[:, c, 0:KC, :], ACT.Square).then_inc(squares_ready, 1)
            with act.Fori(0, NCH) as c:
                act.wait_ge(sums_done, c + 1)
                act.activation(hid[:, c, 2 * KC, :], ps_h[0][:, :], ACT.Sqrt).then_inc(norm_ready, 1)

        @block.vector
        def _(dve):
            def residual(c):
                dve.wait_ge(proj_done, c + 1)
                for oc in range(KC):
                    x_c = xf[:, oc, cols(c * CW, CW)]
                    last = dve.scalar_tensor_tensor(x_c, ps_o[:, oc, :], vec["b_o"][:, oc:oc + 1], x_c,
                                                    ALU.add, ALU.add)
                last.then_inc(o_ready, 1)

            def hidden_stats(c):
                for mt in range(MT):
                    dve.wait_ge(hid_kept, c * MT + mt + 5)
                    last = dve.bn_stats(stats1[:, mt, cols(c * 6, 6)], hid[:, c, mt, :])
                return last

            def batchnorm(blocks, stats, mean, gamma, beta, scale, shift, var_ready, dev_ready, ready, order):
                for m in range(blocks):
                    last = dve.bn_aggr(mean[:, m, :], stats[:, m, :])
                last.then_inc(bn_order, 1)
                dve.wait_ge(bn_order, order + 1)
                dve.tensor_scalar(mean[:, :, 1], mean[:, :, 1], BN_EPS, None, ALU.add).then_inc(var_ready, 1)
                dve.wait_ge(dev_ready, 1)
                dve.reciprocal(scale[:, :], mean[:, :, 1]).then_inc(bn_order, 1)
                dve.wait_ge(bn_order, order + 2)
                dve.tensor_tensor(scale[:, :], scale[:, :], gamma[:, :], ALU.mult).then_inc(bn_order, 1)
                dve.wait_ge(bn_order, order + 3)
                dve.tensor_tensor(shift[:, :], mean[:, :, 0], scale[:, :], ALU.mult).then_inc(bn_order, 1)
                dve.wait_ge(bn_order, order + 4)
                dve.tensor_tensor(shift[:, :], beta[:, :], shift[:, :], ALU.subtract).then_inc(ready, 1)

            dve.wait_ge(vec_loaded, 16 * 8)
            residual(0)
            with dve.Fori(0, NCH - 1) as c:
                residual(c + 1)
                hidden_stats(c)
            hidden_stats(NCH - 1).then_inc(bn_order, 1)
            dve.wait_ge(bn_order, 1)
            batchnorm(MT, stats1, mean1, vec["g_1"], vec["be_1"], scale1, shift1, var1_ready, dev1_ready,
                      bn1_ready, 1)
            with dve.Fori(0, NCH) as c:
                for oc in range(KC):
                    dve.wait_ge(y_kept, c * KC + oc + 1 + KC)
                    dve.bn_stats(stats2[:, oc, cols(c * 6, 6)], hid[:, c, oc, :]).then_inc(xn_order, 1)
            dve.wait_ge(xn_order, NCH * KC)
            batchnorm(KC, stats2, mean2, vec["g_2"], vec["be_2"], scale2, shift2, var2_ready, dev2_ready,
                      bn2_ready, 5)
            with dve.Fori(0, NCH) as c:
                dve.wait_ge(y_scaled, c + 1)
                dve.tensor_tensor(hid[:, c, 0:KC, :], hid[:, c, 0:KC, :], xf[:, :, cols(c * CW, CW)],
                                  ALU.add).then_inc(x1_ready, 1)
            base = NCH * KC
            with dve.Fori(0, NCH) as c:
                norm = hid[:, c, 2 * KC, :]
                dve.wait_ge(norm_ready, c + 2)
                dve.tensor_scalar(norm, norm, 1e-12, None, ALU.max).then_inc(xn_order, 1)
                wait_alone(dve, xn_order, base + c * 2 + 1)
                dve.reciprocal(norm, norm).then_inc(xn_order, 1)
                dve.wait_ge(xn_order, base + c * 2 + 2)
                for kc in range(KC):
                    dve.scalar_tensor_tensor(xf[:, kc, cols(c * CW, CW)], hid[:, c, kc, :],
                                             vec["g_rms"][:, kc:kc + 1], norm, ALU.mult, ALU.mult)
            xn = xf[:, :, :]
            dve.drain()
            dve.tensor_scalar(xn, xn, float(C) ** 0.5, None, ALU.mult).then_inc(xn_ready, 1)
            dve.wait_ge(xn_ready, 1)


def attention_full(nc, cst, xs, w_q, w_k, w_v, ao):
    ctx = ExitStack()
    with ctx:
        sb = lambda name, shape, dt=F32: ctx.enter_context(nc.sbuf_tensor("b_" + name, shape, dt))
        sem = lambda name: ctx.enter_context(nc.semaphore("b_" + name))
        GROUPS, PER = MCH // 2, 2
        ADDED_BY_POOL = 6
        uses = BankUses(plain=3, preparing=6, before=3 * PRE + 3)
        sh = Shared(nc, ctx, cst, xs, "b_", 3, uses, 2)
        v_s = [sb(f"v{n}", [P, MCH, D]) for n in range(2)]
        expo = [sb(f"expo{n}", [P, MCH, PAIR]) for n in range(2)]
        pool_sum = [sb(f"pool_sum{n}", [P, PER, PAIR]) for n in range(2)]
        dve_sum = [sb(f"dve_sum{n}", [P, PER, PAIR]) for n in range(2)]
        row_max = sb("row_max", [P, 2])
        minus_max = [sb(f"minus_max{n}", [P, PAIR], F32R) for n in range(2)]
        parts = sb("parts", [P, 2, PAIR])
        whole = sb("whole", [P, P])
        one_by_sum = sb("one_by_sum", [2 * D, P])

        ps_s = ctx.enter_context(nc.psum_tensor("b_ps_s", [P, 5 * BANK], F32))
        ps_t = [ctx.enter_context(nc.psum_tensor(f"b_ps_t{n}", [P, PER, PAIR], F32)) for n in range(2)]

        scores_done, max_ready, diagonal_ready = sem("scores_done"), sem("max_ready"), sem("diagonal_ready")
        shifted_done, expo_ready = sem("shifted_done"), sem("expo_ready")
        pool_added, dve_added = sem("pool_added"), sem("dve_added")
        one_by_sum_ready = sem("one_by_sum_ready")

        block = ctx.enter_context(nc.Block())

        @block.sync
        def _(sync):
            sh.load_first(sync, w_q, w_k, w_v, None)
            sh.load_and_store(sync, w_q, w_k, w_v, ao,
                              lambda head: sync.wait_ge(sh.o_ready, (head + 1) * PAIRS + 1))

        @block.tensor
        def _(pe):
            def score(tile, u, parity, b, first=False):
                if not first:
                    pe.wait_ge(max_ready, tile)
                for c, n in SCOLS:
                    last = pe.matmul(ps_s[:, c:c + n], sh.q_stack[parity][:, P * u:P * u + P],
                                     sh.k_stack[b][:, c:c + n], start=True, stop=True)
                last.then_inc(scores_done, 1)

            def shifted(pair, g, parity, b):
                bank = ps_t[(parity + g) % 2]
                if g == 0:
                    pe.wait_ge(diagonal_ready, pair + 1)
                pe.wait_ge(expo_ready, pair * GROUPS + g + 1)
                for m in range(PER):
                    block_of_k = sh.k_stack[b][:, P * (PER * g + m):P * (PER * g + m) + P]
                    pe.matmul(bank[:, m, :], cst["ones_r"][:, :], minus_max[parity][:, :], start=True, stop=False)
                    last = pe.matmul(bank[:, m, :], block_of_k, sh.q_stack[parity][:, :], start=False, stop=True)
                last.then_inc(shifted_done, 1)

            def weigh(pair, groups, parity, b):
                for g in groups:
                    pe.wait_ge(expo_ready, pair * GROUPS + g + 3)
                    for m in range(PER * g, PER * g + PER):
                        rows = slice(D * (m % 4), D * (m % 4) + D)
                        pe.matmul(sh.bank[rows, 0:PAIR], v_s[b][:, m, :], expo[parity][:, m, :],
                                  start=m < 4, stop=m + 4 >= MCH)

            def add_up_keys(pair, parity):
                pe.wait_ge(pool_added, (pair + 1) * (ADDED_BY_POOL - 1))
                pe.wait_ge(dve_added, (pair + 1) * (GROUPS - ADDED_BY_POOL - 1))
                for n, t in enumerate((pool_sum[parity], dve_sum[parity])):
                    for m in range(PER):
                        quadrant = PER * n + m
                        last = pe.matmul(sh.bank[D * quadrant:D * quadrant + D, PAIR:2 * PAIR],
                                         cst["ones"][:, 0:D], t[:, m, :], start=True, stop=True)
                last.then_inc(sh.bank_filled, 1)

            pe.wait_ge(sh.wkv_loaded, 80)
            for c in range(PRE):
                sh.project_k(pe, 3 * c, 0, c)
                sh.project_v(pe, 3 * c + 1, 0, c)
                sh.turn_v(pe, 3 * c + 2)
            pe.wait_ge(sh.wq_loaded, 64)
            for n in range(2):
                sh.project_q(pe, 3 * PRE + n, 0, n)
            pe.wait_ge(sh.k_stack_ready, PRE)
            pe.wait_ge(sh.q_stack_ready, 1)
            for u in range(2):
                score(u, u, 0, 0, first=u == 0)
            sh.project_q(pe, 3 * PRE + 2, 0, 2)
            pe.wait_ge(sh.q_stack_ready, 2)
            for g in range(GROUPS):
                shifted(0, g, 0, 0)
                if g in (1, 5):
                    score(2 + g // 5, g // 5, 1, 0)

            def step(pair, i, parity, h, b, head):
                use = uses(head, i)
                tail = isinstance(i, int)
                b_1 = 1 - b if tail and i + 1 >= PAIRS else b
                b_2 = 1 - b if tail and i + 2 >= PAIRS else b
                next_shifted = lambda g: shifted(pair + 1, g, 1 - parity, b_1)
                sh.bank_free(pe, use)
                weigh(pair, range(0, 3), parity, b)
                next_shifted(0)
                weigh(pair, range(3, 6), parity, b)
                next_shifted(1)
                weigh(pair, range(6, 9), parity, b)
                add_up_keys(pair, parity)
                if tail and i + 2 == PAIRS:
                    pe.wait_ge(sh.k_stack_ready, (head + 2) * PRE)
                pe.wait_ge(sh.q_stack_ready, pair + 3)
                score(2 * pair + 4, 0, parity, b_2)
                next_shifted(2)
                sh.bank_free(pe, use + 1)
                for n in range(4):
                    last = pe.matmul(sh.bank[D * n:D * n + D, 0:P], cst["add_up"][:, :],
                                     parts[:, n // 2, P * (n % 2):P * (n % 2) + P], start=True, stop=True)
                last.then_inc(sh.bank_filled, 1)
                next_shifted(3)
                if tail and i + 3 == PAIRS:
                    pe.wait_ge(sh.wq_loaded, 64 * (h + b + 1))
                if tail and i + 3 >= PAIRS:
                    sh.project_q(pe, use + 2, 1 - b, i + 3 - PAIRS)
                else:
                    sh.project_q(pe, use + 2, b, i + 3)
                next_shifted(4)
                if not tail:
                    pe.wait_ge(sh.wkv_loaded, 80 * (h + b + 1))
                    sh.project_k(pe, use + 3, 1 - b, i)
                score(2 * pair + 5, 1, parity, b_2)
                next_shifted(5)
                if not tail:
                    sh.project_v(pe, use + 4, 1 - b, i)
                next_shifted(6)
                if not tail:
                    sh.turn_v(pe, use + 5)
                next_shifted(7)
                next_shifted(8)

            over_steps(pe, step)

        @block.scalar
        def _(act):
            act.sem_inc(expo_ready, 2)
            act.sem_inc(sh.o_ready, 1)

            def keep_turned_v(use, b, c):
                wait_alone(act, sh.bank_filled, use + 1)
                act.activation(v_s[b][:, cols(c * PM, PM), :],
                               sh.bank[:, 0:PM * D].rearrange("p (m d) -> p m d", d=D),
                               ACT.Copy).then_inc(sh.bank_kept, 1)

            def exponentials(pair, g, parity):
                act.wait_ge(shifted_done, pair * GROUPS + g + 1)
                act.activation(expo[parity][:, PER * g:PER * g + PER, :], ps_t[(parity + g) % 2][:, :, :],
                               ACT.Exp, scale=SCALE).then_inc(expo_ready, 1)

            act.wait_ge(sh.buffers_set, 1)
            for c in range(PRE):
                sh.keep_k(act, 3 * c, 0, c)
                sh.keep_v(act, 3 * c + 1, 0)
                keep_turned_v(3 * c + 2, 0, c)
            for n in range(3):
                sh.keep_q(act, 3 * PRE + n, 0, n)
            for g in range(GROUPS):
                exponentials(0, g, 0)

            def step(pair, i, parity, h, b, head):
                use = uses(head, i)
                tail = isinstance(i, int)
                next_exponentials = lambda g: exponentials(pair + 1, g, 1 - parity)
                next_exponentials(0)
                next_exponentials(1)
                act.wait_ge(sh.bank_filled, use + 1)
                act.activation(parts[:, :, :], sh.bank[:, :], ACT.Copy).then_inc(sh.bank_kept, 1)
                next_exponentials(2)
                act.wait_ge(sh.o_ready, pair + 1)
                act.wait_ge(sh.bank_filled, use + 2)
                act.activation(whole[:, :], sh.bank[:, 0:P], ACT.Copy).then_inc(sh.bank_kept, 1)
                next_exponentials(3)
                sh.keep_q(act, use + 2, h + b if tail and i + 3 >= PAIRS else h, pair + 3)
                next_exponentials(4)
                if not tail:
                    sh.keep_k(act, use + 3, h + b, (head + 1) * PRE + i)
                next_exponentials(5)
                if not tail:
                    sh.keep_v(act, use + 4, h + b)
                next_exponentials(6)
                if not tail:
                    keep_turned_v(use + 5, 1 - b, i)
                next_exponentials(7)
                next_exponentials(8)

            over_steps(act, step)

        def add_groups(engine, added, total, pair, groups, parity):
            block_of = lambda g: expo[parity][:, PER * g:PER * g + PER, :]
            for n, g in enumerate(groups[1:]):
                engine.wait_ge(expo_ready, pair * GROUPS + g + 3)
                if n:
                    engine.wait_ge(added, pair * (len(groups) - 1) + n)
                engine.tensor_tensor(total[parity][:, :, :], total[parity][:, :, :] if n else block_of(groups[0]),
                                     block_of(g), ALU.add).then_inc(added, 1)

        @block.gpsimd
        def _(pool):
            def add_up(pair, parity):
                add_groups(pool, pool_added, pool_sum, pair, range(ADDED_BY_POOL), parity)

            for c in range(PRE):
                sh.split_k(pool, 3 * c, 0, c, c + 1)
            for n in range(2):
                sh.split_q(pool, 3 * PRE + n, n, PRE + n + 1)
            add_up(0, 0)
            pool.wait_ge(shifted_done, GROUPS)
            sh.split_q(pool, 3 * PRE + 2, 0, PRE + 3)

            def step(pair, i, parity, h, b, head):
                use = uses(head, i)
                tail = isinstance(i, int)
                splits = PRE + 3 + head * (PAIRS + PRE) + (PRE + i if tail else i * 2)
                add_up(pair + 1, 1 - parity)
                if not tail:
                    sh.split_k(pool, use + 3, 1 - b, i, splits + 1)
                pool.wait_ge(shifted_done, (pair + 2) * GROUPS)
                sh.split_q(pool, use + 2, 1 - parity, splits + (1 if tail else 2))

            over_steps(pool, step)

        @block.vector
        def _(dve):
            def add_up(pair, parity):
                add_groups(dve, dve_added, dve_sum, pair, range(ADDED_BY_POOL, GROUPS), parity)

            def maximum(tile, u):
                dve.wait_ge(scores_done, tile + 1)
                dve.tensor_reduce(row_max[:, u:u + 1], ps_s[:, 0:N], AX.X, ALU.max).then_inc(max_ready, 1)

            def diagonals(pair, parity):
                dve.wait_ge(max_ready, 2 * pair + 2)
                for u in range(2):
                    last = dve.tensor_scalar(minus_max[parity][:, P * u:P * u + P], cst["ident"][:, :],
                                             row_max[:, u:u + 1], -1.0, ALU.mult, ALU.mult)
                last.then_inc(diagonal_ready, 1)

            for t in (sh.bq_s, sh.bk_s, sh.bv_s):
                last = dve.memset(t[:, :], 0.0)
            last.then_inc(sh.buffers_set, 1)
            for pair in range(2):
                for u in range(2):
                    maximum(2 * pair + u, u)
                diagonals(pair, pair)
            add_up(0, 0)

            def step(pair, i, parity, h, b, head):
                use = uses(head, i)
                maximum(2 * pair + 4, 0)
                wait_alone(dve, sh.bank_kept, use + 2)
                dve.reciprocal(one_by_sum[:, :], whole[2 * D:4 * D, :]).then_inc(one_by_sum_ready, 1)
                maximum(2 * pair + 5, 1)
                wait_alone(dve, sh.o_stored, 16 * (head + 1))
                dve.wait_ge(one_by_sum_ready, pair + 1)
                for u in range(2):
                    rows = slice(D * u, D * u + D)
                    last = dve.tensor_tensor(sh.o_head[b][:, cols(i * PAIR + P * u, P)], whole[rows, :],
                                             one_by_sum[rows, :], ALU.mult)
                last.then_inc(sh.o_ready, 1)
                diagonals(pair + 2, parity)
                add_up(pair + 1, 1 - parity)

            over_steps(dve, step)


def output(nc, xs, ao, x1, w_out, b_out, out):
    CW = N // PRE
    CHB = N // CW
    ctx = ExitStack()
    with ctx:
        sb = lambda name, shape, dt=F32: ctx.enter_context(nc.sbuf_tensor("o_" + name, shape, dt))
        sem = lambda name: ctx.enter_context(nc.semaphore("o_" + name))
        w, bias = sb("w", [P, KC, C]), sb("bias", [P, KC])
        a, y = sb("a", [P, KC, B * N]), sb("y", [P, KC, B * N])
        ps = ctx.enter_context(nc.psum_tensor("o_ps", [P, KC, BANK], F32))
        w_loaded, a_loaded = sem("w_loaded"), [sem(f"a_loaded{b}") for b in range(B)]
        proj_done, added, stored = sem("proj_done"), sem("added"), sem("stored")
        block = ctx.enter_context(nc.Block())

        @block.sync
        def _(sync):
            sync.dma_start(w[:, :, :], w_out.rearrange("(k p) o -> p k o", p=P)).then_inc(w_loaded, 16)
            sync.dma_start(bias[:, :], b_out).then_inc(w_loaded, 16)
            for b in range(B):
                for kc in range(KC):
                    for t, src in ((a, ao), (y, x1)):
                        sync.dma_start(t[:, kc, b * N:b * N + N],
                                       src[kc * P:kc * P + P, b * N:b * N + N]).then_inc(a_loaded[b], 16)
            for b in range(B):
                with sync.Fori(0, CHB) as c:
                    sync.wait_ge(added, c + b * CHB + 2)
                    sync.dma_start(out[b].rearrange("(k p) n -> p k n", p=P)[:, :, cols(c * CW, CW)],
                                   y[:, :, cols(c * CW + b * N, CW)]).then_inc(stored, 16)
            sync.wait_ge(stored, 16 * B * CHB)

        @block.tensor
        def _(pe):
            pe.sem_inc(added, 1)
            pe.wait_ge(w_loaded, 32)
            for b in range(B):
                pe.wait_ge(a_loaded[b], 64)
                with pe.Fori(0, CHB) as c:
                    pe.wait_ge(added, c + b * CHB + 1)
                    for oc in range(KC):
                        for kc in range(KC):
                            last = pe.matmul(ps[:, oc, 0:CW], w[:, kc, P * oc:P * oc + P],
                                             a[:, kc, cols(c * CW + b * N, CW)], start=kc == 0, stop=kc == KC - 1)
                    last.then_inc(proj_done, 1)

        @block.vector
        def _(dve):
            dve.wait_ge(w_loaded, 32)
            for b in range(B):
                dve.wait_ge(a_loaded[b], 64)
                with dve.Fori(0, CHB) as c:
                    dve.wait_ge(proj_done, c + b * CHB + 1)
                    for oc in range(KC):
                        y_c = y[:, oc, cols(c * CW + b * N, CW)]
                        last = dve.scalar_tensor_tensor(y_c, ps[:, oc, 0:CW], bias[:, oc:oc + 1], y_c,
                                                        ALU.add, ALU.add)
                    last.then_inc(added, 1)


def build(nc, t, out):
    ao0 = nc.dram_tensor("ao0", [C, B * N], F32).ap()
    x1 = nc.dram_tensor("x1", [C, B * N], F32).ap()
    ao1 = nc.dram_tensor("ao1", [C, B * N], F32).ap()
    ctx = ExitStack()
    with ctx:
        xs = ctx.enter_context(nc.sbuf_tensor("xs", [P, KC, B, N], F32))
        cst = constants(nc, ctx)
        attention_top(nc, cst, xs, t["x"], t["w_q0"], t["w_k0"], t["w_v0"], t["b_q"], t["b_k"], t["b_v"], ao0)
        mlp(nc, cst, xs, ao0, x1, t["w_o"], t["b_o"], t["w_1"], t["b_1"], t["g_1"], t["be_1"],
            t["w_2"], t["b_2"], t["g_2"], t["be_2"], t["g_rms"])
        attention_full(nc, cst, xs, t["w_q1"], t["w_k1"], t["w_v1"], ao1)
        output(nc, xs, ao1, x1, t["w_out"], t["b_out"], out)


def per_head(w):
    return np.ascontiguousarray(w.reshape(HEADS, D, KC, P).transpose(0, 3, 2, 1))


def per_partition(v, rows=P):
    return np.ascontiguousarray(v.reshape(-1, rows).T)


def kernel(**inputs):
    from concourse import bacc
    from concourse.bass_utils import run_bass_kernel_spmd

    a = {name: np.asarray(v) for name, v in inputs.items()}
    layer0 = {name[len("L0_conv_"):]: v for name, v in a.items() if name.startswith("L0_conv_")}
    qkv = a["L1_conv_w_qkv"]
    arrays = {
        "x": a["x"].reshape(B, C, N),
        "w_q0": per_head(layer0["Wq"]), "w_k0": per_head(layer0["Wk"]), "w_v0": per_head(layer0["Wv"]),
        "b_q": per_partition(layer0["bq"], D), "b_k": per_partition(layer0["bk"], D),
        "b_v": per_partition(layer0["bv"], D),
        "w_o": layer0["Wo"].T, "b_o": per_partition(layer0["bo"]),
        "w_1": layer0["W1"].T, "b_1": per_partition(layer0["b1"]),
        "g_1": per_partition(layer0["g1"]), "be_1": per_partition(layer0["be1"]),
        "w_2": layer0["W2"].T, "b_2": per_partition(layer0["b2"]),
        "g_2": per_partition(layer0["g2"]), "be_2": per_partition(layer0["be2"]),
        "g_rms": per_partition(a["L1_conv_g"]),
        "w_q1": per_head(qkv[0:C]), "w_k1": per_head(qkv[C:2 * C]), "w_v1": per_head(qkv[2 * C:3 * C]),
        "w_out": a["L1_conv_w_out"].T, "b_out": per_partition(a["L1_conv_b_out"]),
    }
    arrays = {name: np.ascontiguousarray(v) for name, v in arrays.items()}
    nc = bacc.Bacc("TRN2", target_bir_lowering=False, num_devices=1)
    t = {name: nc.dram_tensor(name, v.shape, F32, kind="ExternalInput").ap() for name, v in arrays.items()}
    out = nc.dram_tensor("out", [B, C, N], F32, kind="ExternalOutput").ap()
    build(nc, t, out)
    result = run_bass_kernel_spmd(nc, [arrays], core_ids=[0])
    return result.results[0]["out"].reshape(B, C, 48, 48)
```
